# Optimizing a Trainium2 kernel written in Bass

```python
import numpy as np
import jax
import jax.numpy as jnp

def _softmax(x, axis=-1):
    return jax.nn.softmax(x, axis=axis)

def _gelu(x):
    return jax.nn.gelu(x, approximate=True)

def _silu(x):
    return jax.nn.silu(x)

def _sigmoid(x):
    return jax.nn.sigmoid(x)

def _layernorm(x, axis=-1, eps=1e-05):
    m = jnp.mean(x, axis=axis, keepdims=True)
    v = jnp.var(x, axis=axis, keepdims=True)
    return (x - m) / jnp.sqrt(v + eps)

def _scatter_add(tgt, idx, src, axis=0):
    return tgt.at[idx].add(src)

def _segment_sum(src, seg, n):
    return jax.ops.segment_sum(src, seg, n)
kernel_name = 'mk_gnn_resnorm_d2_gnn_r32_dc1c50'

def setup_inputs(seed: int=0):
    np.random.seed(seed)
    _w = jnp.asarray

    def _rec_inputs():
        import jax
        import jax.numpy as jnp
        _gk = jax.random.key(seed)
        x = -0.000202 + 1 * jax.random.normal(jax.random.fold_in(_gk, 1), (3125, 64), jnp.float32)
        _s = jax.random.randint(jax.random.fold_in(_gk, 2), (50000,), 0, 3125, jnp.int32)
        _d = jax.random.randint(jax.random.fold_in(_gk, 3), (50000,), 0, 3125, jnp.int32)
        _loop = jnp.arange(3125, dtype=jnp.int32)
        src = jnp.concatenate([_s, _d, _loop])
        dst = jnp.concatenate([_d, _s, _loop])
        _o = jnp.argsort(dst, stable=True)
        src = src[_o]
        dst = dst[_o]
        edge_type_32 = jax.random.randint(jax.random.fold_in(_gk, 12), (103125,), 0, 32, jnp.int32)
        return (x, src, dst, edge_type_32)
    x, src, dst, edge_type_32 = _rec_inputs()

    def _L0_gnn_setup():
        import jax, jax.numpy as jnp
        import numpy as np
        N_NODES = 3125
        N_EDGES = 50000
        D_IN = 64
        D_OUT = 64
        K_HOPS = 2
        key = jax.random.key(seed)
        k1, k2, k3, k4 = jax.random.split(key, 4)
        x = jax.random.normal(k1, (N_NODES, D_IN), dtype=jnp.float32)
        W = jax.random.normal(k2, (D_OUT, D_IN), dtype=jnp.float32) * (1.0 / np.sqrt(D_IN))
        b = jax.random.normal(k3, (D_OUT,), dtype=jnp.float32) * 0.01
        edge_index = jax.random.randint(k4, (2, N_EDGES), 0, N_NODES, dtype=jnp.int64)
        return {'x': x, 'W': W, 'b': b, 'edge_index': edge_index}
    _L0_gnn_all = _L0_gnn_setup()
    _L0_gnn_in = {k: v for k, v in _L0_gnn_all.items() if k in ('W', 'b')}
    del _L0_gnn_all

    def _L1_gnn_setup():
        import jax, jax.numpy as jnp
        import numpy as np
        N_NODES = 50000
        N_EDGES = 25000
        IN_F = 64
        OUT_F = 64
        N_REL = 32
        N_BASES = 30
        key = jax.random.key(seed)
        ks = jax.random.split(key, 6)
        x = jax.random.normal(ks[0], (N_NODES, IN_F), dtype=jnp.float32)
        edge_index = jax.random.randint(ks[1], (2, N_EDGES), 0, N_NODES, dtype=jnp.int64)
        edge_type = jax.random.randint(ks[2], (N_EDGES,), 0, N_REL, dtype=jnp.int64)
        basis = jax.random.normal(ks[3], (N_BASES, IN_F, OUT_F), dtype=jnp.float32) * 0.01
        coeff = jax.random.normal(ks[4], (N_REL, N_BASES), dtype=jnp.float32) * 0.01
        self_weight = jax.random.normal(ks[5], (IN_F, OUT_F), dtype=jnp.float32) * 0.01
        bias = jnp.zeros((OUT_F,), dtype=jnp.float32)
        return {'x': x, 'edge_index': edge_index, 'edge_type': edge_type, 'num_nodes': N_NODES, 'basis': basis, 'coeff': coeff, 'self_weight': self_weight, 'bias': bias}
    _L1_gnn_all = _L1_gnn_setup()
    _L1_gnn_in = {k: v for k, v in _L1_gnn_all.items() if k in ('basis', 'coeff', 'self_weight', 'bias')}
    del _L1_gnn_all
    return {'x': x, 'src': src, 'dst': dst, 'edge_type_32': edge_type_32, 'L0_gnn_W': _L0_gnn_in['W'], 'L0_gnn_b': _L0_gnn_in['b'], 'L1_gnn_basis': _L1_gnn_in['basis'], 'L1_gnn_coeff': _L1_gnn_in['coeff'], 'L1_gnn_self_weight': _L1_gnn_in['self_weight'], 'L1_gnn_bias': _L1_gnn_in['bias']}

def reference(x, src, dst, edge_type_32, L0_gnn_W, L0_gnn_b, L1_gnn_basis, L1_gnn_coeff, L1_gnn_self_weight, L1_gnn_bias):
    import jax
    import jax.numpy as jnp

    def _L0_gnn_ref(x, W, b, edge_index):
        import jax, jax.numpy as jnp
        import numpy as np
        N_NODES = 3125
        N_EDGES = 50000
        D_IN = 64
        D_OUT = 64
        K_HOPS = 2
        n = x.shape[0]
        self_loops = jnp.arange(n, dtype=edge_index.dtype)
        row = jnp.concatenate([edge_index[0], self_loops])
        col = jnp.concatenate([edge_index[1], self_loops])
        ones = jnp.ones(row.shape[0], dtype=x.dtype)
        deg = jax.ops.segment_sum(ones, col, num_segments=n)
        deg_inv_sqrt = jnp.where(deg > 0, jax.lax.rsqrt(deg), 0.0).astype(x.dtype)
        norm = deg_inv_sqrt[row] * deg_inv_sqrt[col]
        h = x
        for _ in range(K_HOPS):
            h = jax.ops.segment_sum(norm[:, None] * h[row], col, num_segments=n)
        out = h @ W.T + b
        return jax.nn.relu(out)

    def _L1_gnn_ref(x, edge_index, edge_type, num_nodes, basis, coeff, self_weight, bias):
        import jax, jax.numpy as jnp
        import numpy as np
        N_NODES = 50000
        N_EDGES = 25000
        IN_F = 64
        OUT_F = 64
        N_REL = 32
        N_BASES = 30
        rel_weight = jnp.einsum('rb,bio->rio', coeff, basis)
        source_idx = edge_index[0]
        target_idx = edge_index[1]
        src_feats = x[source_idx]

        def body(out, rw_r):
            rw, r = rw_r
            mask = (edge_type == r).astype(jnp.float32)
            msg = src_feats @ rw * mask[:, None]
            return (out.at[target_idx].add(msg), None)
        out0 = jnp.zeros((num_nodes, rel_weight.shape[-1]), dtype=jnp.float32)
        out, _ = jax.lax.scan(body, out0, (rel_weight, jnp.arange(rel_weight.shape[0])))
        in_degree = jnp.zeros((num_nodes,), dtype=jnp.float32).at[target_idx].add(1.0)
        in_degree = jnp.maximum(in_degree, 1.0)
        out = out / in_degree[:, None]
        out = out + x @ self_weight + bias
        return out
    edge_index = jnp.stack([src, dst])
    x = _layernorm(x + _L0_gnn_ref(x, L0_gnn_W, L0_gnn_b, edge_index), axis=-1)
    x = _layernorm(x + _L1_gnn_ref(x, edge_index, edge_type_32, 3125, L1_gnn_basis, L1_gnn_coeff, L1_gnn_self_weight, L1_gnn_bias), axis=-1)
    return x

_drawn_inputs = setup_inputs


def setup_inputs(seed=0):
    import zlib

    import numpy as np

    out = dict(_drawn_inputs(seed))
    spreads = {'L1_gnn_bias': (0.0, 0.1)}
    factors = {'L0_gnn_b': 8.0, 'L1_gnn_basis': 8.0, 'L1_gnn_coeff': 8.0}
    for name, (base, spread) in spreads.items():
        noise = np.random.default_rng([zlib.crc32(name.encode()), seed]).standard_normal(out[name].shape)
        drawn = base * np.exp(spread * noise) if base else spread * noise
        out[name] = jnp.asarray(drawn.astype(out[name].dtype))
    for name, factor in factors.items():
        out[name] = (out[name] * factor).astype(out[name].dtype)
    return out
```

```python
from contextlib import ExitStack

import concourse.bass as bass
from concourse import mybir

N, D, E, R, B = 3125, 64, 103125, 32, 30
LO, HI = 125, 25
P = 128
J = 4
GE = J * P
NG = -(-E // GE)
C = -(-NG // P)
GP = C * P
NPAIR = NG // 2
W = 18
KW = W * HI
ND = N + 19
Q2 = 2
KW2 = Q2 * LO
ROUND = 12582912.0
FAR = -1048576.0
EPS = 1e-5
KEYS, LOS, KEY2, ROWS = range(4)


def build(nc, x, src, dst, typ, w, b, basis, coeff, selfw, bias, out):
    fp32, i32 = mybir.dt.float32, mybir.dt.int32
    bf16, fp16 = mybir.dt.bfloat16, mybir.dt.float16
    ALU, ACT, AX = mybir.AluOpType, mybir.ActivationFunctionType, mybir.AxisListType
    ctx = ExitStack()
    with ctx:
        def sb(name, shape, dt):
            return ctx.enter_context(nc.sbuf_tensor(name, shape, dt))

        def sem(name):
            return ctx.enter_context(nc.semaphore(name))

        rel_dram = nc.dram_tensor("rel_dram", (R, D, D), fp32, kind="Internal").ap()
        table = nc.dram_tensor("table", (N * R, D), fp32, kind="Internal").ap()

        adj = sb("adj", [P, HI, ND], bf16)
        adj_flat = adj[:, :, :].rearrange("p h n -> p (h n)")

        def inside(first_hi, words, dt=fp32):
            start = first_hi * ND
            return adj_flat[:, start:start + 2 * words].bitcast(dt)

        TM = C * GE
        TAIL = 12
        def tm(n, dt=fp32):
            start = 18 * ND + n * 2 * TM
            return adj_flat[:, start:start + 2 * TM].bitcast(dt)
        raw = [tm(n, i32) for n in range(3)]
        srcF, dstF, typF, hiF, keyF, key2F = (tm(n) for n in range(3, 9))
        eid = adj_flat[:, 18 * ND + 9 * 2 * TM:18 * ND + 9 * 2 * TM + 2 * GE].bitcast(fp32)
        basis_sb = inside(12, D * D)
        rel_sb = inside(15, D * D)
        oh2 = inside(0, 2 * J * KW2).rearrange("p (s j k) -> p s j k", s=2, j=J)
        got = inside(3, 2 * J * D).rearrange("p (s j d) -> p s j d", s=2, j=J)
        acc = inside(4, (HI + Q2) * D)
        y = inside(7, HI * D).rearrange("p (h d) -> p h d", h=HI)
        iota_2 = inside(9, KW2)
        y2 = inside(10, HI * D).rearrange("p (h d) -> p h d", h=HI)

        split1 = sb("split1", [P, HI, 3 * D], bf16)
        rel = split1[0:D, :, :].rearrange("p h d -> p (h d)")[:, 0:2 * (R + 1) * D].bitcast(fp32)
        xT = split1[0:D, :, :].rearrange("p h d -> p (h d)")[:, 0:2 * J * P * 2].bitcast(fp32).rearrange("p (s n) -> p s n", s=2)
        u1 = sb("u1", [P, HI * 3 * D], bf16)
        split2 = u1[:, :].rearrange("p (h d) -> p h d", h=HI)
        keys = u1[:, 0:2 * J * GP].bitcast(fp32).rearrange("p (j g) -> p j g", j=J)
        los = u1[:, 2 * J * GP:4 * J * GP].bitcast(fp32).rearrange("p (j g) -> p j g", j=J)
        key2 = sb("key2", [P, J, GP], fp32)
        rows = sb("rows", [P, J, GP], fp32)
        prop = sb("prop", [P, HI, D], fp32)
        xs = sb("xs", [P, HI, D], fp32)
        u2 = sb("u2", [P, 2 * J * (KW + P)], bf16)
        ohk = u2[:, 0:2 * J * KW].rearrange("p (s j k) -> p s j k", s=2, j=J)
        ohl = u2[:, 2 * J * KW:].rearrange("p (s j k) -> p s j k", s=2, j=J)
        stage = u2[:, 0:4 * 2 * 512].bitcast(fp32).rearrange("p (s n) -> p s n", s=4)
        iota_k = sb("iota_k", [P, KW], fp16)
        ident = sb("ident", [P, P], fp32)
        ones = sb("ones", [P, 1], bf16)
        bvec = sb("bvec", [P, D], fp32)
        biasvec = sb("biasvec", [P, D], fp32)
        head = u1[:, 0:2 * (2 * D + B + R)].bitcast(fp32)
        wt, wsb = head[0:D, 0:D], head[0:D, D:2 * D]
        cfsb, cft = head[0:R, 2 * D:2 * D + B], head[0:B, 2 * D + B:]
        sm = sb("sm", [P, 6], fp32)
        sm2 = sb("sm2", [P, 6], fp32)
        tabl = sb("tabl", [1, 2 * GP], i32)
        cnts = sb("cnts", [1, 2], fp32)
        passes = sb("passes", [1, 2], i32)
        dinv = sb("dinv", [P, HI], fp32)
        dinv2 = sb("dinv2", [P, HI], fp32)
        rind = sb("rind", [P, HI], fp32)
        deg = sb("deg", [P, HI], fp32)
        tmp = sb("tmp", [P, 3, D], fp32)
        x1 = sb("x1", [P, 2, D], fp32)
        x1T = u2[0:D, 4 * 2 * 512:4 * 2 * 512 + 4 * P].bitcast(fp32).rearrange("p (s n) -> p s n", s=2)
        stats = sb("stats", [P, 6], fp32)
        mv = sb("mv", [P, 2], fp32)
        rstd = sb("rstd", [P, 2], fp32)
        idx = sb("idx", [P, 2, J], i32)
        mean = inside(6, 2 * HI)[:, 0:HI]
        var = inside(6, 2 * HI)[:, HI:]
        epsv = sb("epsv", [P, 1], fp32)
        ps = ctx.enter_context(nc.psum_tensor("ps", [P, 8, 512], fp32))

        s_src, s_dst, s_typ = sem("s_src"), sem("s_dst"), sem("s_typ")
        s_pad = sem("s_pad")
        s_x, s_small, s_basis, s_self, s_rel, s_relw, s_bias = (sem(n) for n in ("s_x", "s_small", "s_basis", "s_self", "s_rel", "s_relw", "s_bias"))
        s_c0, s_ident, s_const, s_eid = (sem(n) for n in ("s_c0", "s_ident", "s_const", "s_eid"))
        s_head, s_wt, s_relps, s_relsb, s_xT, s_xTs, s_xw, s_xws = (sem(n) for n in ("s_head", "s_wt", "s_relps", "s_relsb", "s_xT", "s_xTs", "s_xw", "s_xws"))
        d_step = sem("d_step")
        s_keysF, s_keyT, s_keysb, s_rowT, s_rows, s_zero = (sem(n) for n in ("s_keysF", "s_keyT", "s_keysb", "s_rowT", "s_rows", "s_zero"))
        oh_ready, oh_free, win_done, win_free = (sem(n) for n in ("oh_ready", "oh_free", "win_done", "win_free"))
        s_deg, s_prop, s_hop, s_hopfree, s_split2, s_var, s_std = (sem(n) for n in ("s_deg", "s_prop", "s_hop", "s_hopfree", "s_split2", "s_var", "s_std"))
        s_x1, s_x1ps, s_x1T, s_y, s_ysb, s_selfps, s_selfsb = (sem(n) for n in ("s_x1", "s_x1ps", "s_x1T", "s_y", "s_ysb", "s_selfps", "s_selfsb"))
        s_yout = [sem(f"s_yout{i}") for i in range(4)]
        s_adjfree, s_accz, slot_taken = sem("s_adjfree"), sem("s_accz"), sem("slot_taken")
        oh2_ready, oh2_free, msg_done, msg_free, idx_ready, idx_free = (sem(n) for n in ("oh2_ready", "oh2_free", "msg_done", "msg_free", "idx_ready", "idx_free"))
        s_got = [sem(f"s_got{i}") for i in range(2)]
        s_fv, s_fs, s_fin, s_out = sem("s_fv"), sem("s_fs"), sem("s_fin"), sem("s_out")

        block = ctx.enter_context(nc.Block())
        FULL = E // GE
        TOP = FULL - P
        LAST = E - FULL * GE

        @block.sync
        def _(sp):
            sp.wait_ge(s_pad, 3)
            for a, r, s in ((dst, raw[1], s_dst), (src, raw[0], s_src), (typ, raw[2], s_typ)):
                v = r.rearrange("p (c e) -> p c e", c=C)
                sp.dma_start(v[:, 0, :], a[0:P * GE].rearrange("(p e) -> p e", p=P)).then_inc(s, 16)
                sp.dma_start(v[0:TOP, 1, :], a[P * GE:FULL * GE].rearrange("(p e) -> p e", e=GE)).then_inc(s, 16)
                sp.dma_start(v[TOP:TOP + 1, 1, 0:LAST], a[FULL * GE:E].rearrange("(p e) -> p e", p=1)).then_inc(s, 16)
            sp.wait_ge(s_relsb, 8)
            sp.dma_start(rel_dram.rearrange("r i o -> r (i o)"), rel_sb[0:R, :]).then_inc(s_relw, 16)
            sp.wait_ge(s_relw, 16)
            sp.wait_ge(s_hop, HI)
            sp.dma_start(rel[:, 0:R * D].rearrange("i (r o) -> i r o", r=R), rel_dram.rearrange("r i o -> i r o")).then_inc(s_rel, 16)
            sp.dma_start(rel[:, R * D:(R + 1) * D], selfw).then_inc(s_rel, 16)
            tv = table.rearrange("(n r) d -> n (r d)", r=R)
            for q in range(HI):
                for c in range(4):
                    sp.wait_ge(s_ysb, 4 * q + c + 1)
                    sp.dma_start(tv[q * LO:(q + 1) * LO, c * 512:(c + 1) * 512], stage[0:LO, c, :]).then_inc(s_yout[c], 16)
            sp.wait_ge(s_fin, 1)
            sp.dma_start(out.rearrange("(h l) d -> l h d", l=LO), y[0:LO, :, :]).then_inc(s_out, 16)
            sp.wait_ge(s_out, 16)

        @block.gpsimd
        def _(pool):
            pool.memset(raw[0], 0).then_inc(s_pad, 1)
            pool.memset(raw[1], N - 1).then_inc(s_pad, 1)
            pool.memset(raw[2], 0).then_inc(s_pad, 1)
            pool.memset(ident[:], 0.0).then_inc(s_c0, 1)
            pool.wait_ge(s_c0, 1)
            pool.affine_select(out=ident[:], in_=ident[:], compare_op=ALU.not_equal, fill=1.0, base=0,
                               pattern=[[-1, P]], channel_multiplier=1).then_inc(s_ident, 1)
            pool.iota(eid, [[1, GE]], base=P * GE - E, channel_multiplier=GE,
                      allow_small_or_imprecise_dtypes=True).then_inc(s_eid, 1)
            pool.iota(iota_k[:], [[1, KW]], base=0, channel_multiplier=0, allow_small_or_imprecise_dtypes=True).then_inc(s_const, 1)
            pool.memset(ones[:], 1.0).then_inc(s_const, 1)
            pool.memset(epsv[:], EPS).then_inc(s_const, 1)
            pool.memset(inside(0, TAIL * ND // 2), 0.0).then_inc(s_zero, 1)
            pool.wait_ge(s_keyT, 8)
            pool.wait_ge(s_relw, 16)
            pool.memset(inside(TAIL, 5 * ND // 2), 0.0).then_inc(s_zero, 1)

            pool.wait_ge(s_rows, 1)
            m2 = pool.value_load(passes[0:1, 1:2], min_val=1, max_val=N)
            for c in range(4):
                pool.wait_ge(s_yout[c], 16 * HI)
            pool.iota(iota_2, [[1, KW2]], base=0, channel_multiplier=0, allow_small_or_imprecise_dtypes=True).then_inc(s_const, 1)
            with pool.Fori(0, m2) as v:
                with pool.Fori(0, NPAIR) as i:
                    for s in range(2):
                        pool.wait_ge(idx_ready, v * NG + i * 2 + s + 1)
                        pool.wait_ge(oh2_free, v * NG + i * 2 + s + 1)
                        pool.sem_inc(slot_taken, 1)
                        for j in range(J):
                            pool.indirect_dma_start(got[:, s, j, :], None, table,
                                                    bass.IndirectOffsetOnAxis(ap=idx[:, s, j:j + 1], axis=0)).then_inc(s_got[s], 16)

        @block.scalar
        def _(act):
            act.dma_start(wsb, w).then_inc(s_small, 16)
            act.dma_start(cfsb, coeff).then_inc(s_small, 16)
            act.dma_start(xs[0:LO, :, :], x.rearrange("(h l) d -> l h d", l=LO)).then_inc(s_x, 16)
            act.dma_start(basis_sb[0:B, :], basis.rearrange("b i o -> b (i o)")).then_inc(s_basis, 16)
            act.dma_start(bvec[:], b[None, :].to_broadcast([P, D])).then_inc(s_bias, 16)
            act.dma_start(biasvec[:], bias[None, :].to_broadcast([P, D])).then_inc(s_bias, 16)
            act.wait_ge(s_head, 2)
            act.copy(wt, ps[0:D, 0, 0:D]).then_inc(s_wt, 1)
            act.copy(cft, ps[0:B, 1, 0:R]).then_inc(s_wt, 1)
            for k in range(8):
                act.wait_ge(s_relps, k + 1)
                act.copy(rel_sb[0:R, k * 512:(k + 1) * 512], ps[0:R, 2 + k % 2, :]).then_inc(s_relsb, 1)
            for k in range(7):
                n = min(4, HI - 4 * k)
                act.wait_ge(s_xT, k + 1)
                if k >= 2:
                    act.wait_ge(s_xw, k - 1)
                act.copy(xT[:, k % 2, 0:n * LO], ps[0:D, 4 + k % 2, 0:n * LO]).then_inc(s_xTs, 1)
                act.wait_ge(s_xw, k + 1)
                act.copy(prop[0:LO, 4 * k:4 * k + n, :], ps[0:LO, 6 + k % 2, 0:n * D].rearrange("p (n d) -> p n d", n=n)).then_inc(s_xws, 1)
            act.wait_ge(s_var, 1)
            act.wait_ge(s_const, 3)
            act.activation(dinv[:], deg[:], ACT.Sqrt).then_inc(s_std, 1)
            for q in range(HI):
                act.wait_ge(s_var, q + 2)
                act.activation(rstd[0:LO, q % 2:q % 2 + 1], mv[0:LO, 1:2], ACT.Sqrt, bias=epsv[0:LO, :]).then_inc(s_std, 1)
                act.wait_ge(s_x1ps, q + 1)
                act.copy(x1T[:, q % 2, 0:LO], ps[0:D, 2, 0:LO]).then_inc(s_x1T, 1)
                for c in range(4):
                    act.wait_ge(s_y, 4 * q + c + 1)
                    if q >= 1:
                        act.wait_ge(s_yout[c], 16 * q)
                    act.copy(stage[0:LO, c, :], ps[0:LO, 3 + c, :]).then_inc(s_ysb, 1)
            act.wait_ge(s_rows, 1)
            m2 = act.value_load(passes[0:1, 1:2], min_val=1, max_val=N)
            act.wait_ge(s_keysb, 4)
            with act.Fori(0, m2) as v:
                with act.Fori(0, NPAIR) as i:
                    for s in range(2):
                        act.wait_ge(oh2_free, v * NG + i * 2 + s + 1)
                        act.copy(idx[:, s, :], rows[:, :, bass.ds(i * 2 + s, 1)].rearrange("p j o -> p (j o)")).then_inc(idx_ready, 1)
            act.wait_ge(s_fv, 1)
            act.activation(var[0:LO, :], var[0:LO, :], ACT.Sqrt, bias=epsv[0:LO, :], scale=1.0 / D).then_inc(s_fs, 1)

        @block.tensor
        def _(pe):
            pe.wait_ge(s_ident, 1)
            pe.wait_ge(s_small, 32)
            pe.transpose(ps[0:D, 0, 0:D], wsb, ident[0:D, 0:D]).then_inc(s_head, 1)
            pe.transpose(ps[0:B, 1, 0:R], cfsb, ident[0:R, 0:R]).then_inc(s_head, 1)
            pe.wait_ge(s_wt, 2)
            pe.wait_ge(s_basis, 16)
            for k in range(8):
                if k >= 2:
                    pe.wait_ge(s_relsb, k - 1)
                pe.matmul(ps[0:R, 2 + k % 2, :], cft, basis_sb[0:B, k * 512:(k + 1) * 512], start=True, stop=True).then_inc(s_relps, 1)
            pe.wait_ge(s_x, 16)

            def x_transpose(k):
                n = min(4, HI - 4 * k)
                if k >= 2:
                    pe.wait_ge(s_xTs, k - 1)
                for m in range(n):
                    last = pe.transpose(ps[0:D, 4 + k % 2, m * LO:(m + 1) * LO], xs[0:LO, 4 * k + m, :], ident[0:LO, 0:LO])
                last.then_inc(s_xT, 1)

            x_transpose(0)
            for k in range(7):
                if k < 6:
                    x_transpose(k + 1)
                n = min(4, HI - 4 * k)
                pe.wait_ge(s_xTs, k + 1)
                if k >= 2:
                    pe.wait_ge(s_xws, k - 1)
                for m in range(n):
                    last = pe.matmul(ps[0:LO, 6 + k % 2, m * D:(m + 1) * D], xT[:, k % 2, m * LO:(m + 1) * LO], wt, start=True, stop=True)
                last.then_inc(s_xw, 1)
            pe.wait_ge(s_xws, 7)
            pe.wait_ge(s_keysF, 1)
            for k in range(6):
                last = pe.transpose(ps[0:1, k // 4, (k % 4) * P:(k % 4 + 1) * P], sm[:, k:k + 1], ident[:])
            last.then_inc(s_rowT, 1)
            for k, (arr, need) in enumerate(((srcF, 2), (typF, 2), (keyF, 3), (key2F, 3))):
                pe.wait_ge(s_keysF, need)
                v = arr.rearrange("p (c j e) -> p c j e", c=C, j=J)
                for c in range(C):
                    t = 2 + (2 * k + c) % 6
                    if 2 * k + c >= 6:
                        pe.wait_ge(s_keysb, 1)
                    for j in range(J):
                        last = pe.transpose(ps[:, t, j * P:(j + 1) * P], v[:, c, j, :], ident[:])
                    last.then_inc(s_keyT, 1)

            pe.wait_ge(s_rows, 1)
            m1 = pe.value_load(passes[0:1, 0:1], min_val=1, max_val=N)
            pe.wait_ge(s_keysb, 4)
            with pe.Fori(0, m1) as v:
                with pe.Fori(0, NPAIR) as i:
                    for s in range(2):
                        pe.wait_ge(oh_ready, v * NG + i * 2 + s + 1)
                        pe.wait_ge(win_free, v * NG + i * 2 + s + 1)
                        for j in range(J):
                            last = pe.matmul(ps[:, s, 0:KW], ohl[:, s, j, :], ohk[:, s, j, :], start=(j == 0), stop=(j == J - 1))
                        last.then_inc(win_done, 1)
            pe.wait_ge(s_prop, 1)
            for q in range(HI):
                for h in range(HI):
                    last = pe.matmul(ps[0:LO, 2, q:q + 1], adj[:, h, q * LO:(q + 1) * LO], ones[:], start=(h == 0), stop=(h == HI - 1))
            last.then_inc(s_deg, 1)

            def hop(q, parts, n):
                if n >= 2:
                    pe.wait_ge(s_hopfree, n - 1)
                for h in range(HI):
                    last = pe.matmul(ps[0:LO, n % 2, 0:3 * D], adj[:, h, q * LO:(q + 1) * LO], parts[:, h, :], start=(h == 0), stop=(h == HI - 1))
                last.then_inc(s_hop, 1)

            pe.wait_ge(s_prop, 2)
            for q in range(HI):
                hop(q, split1, q)
            pe.wait_ge(s_split2, HI)
            hop(0, split2, HI)
            for q in range(HI):
                if q < HI - 1:
                    hop(q + 1, split2, HI + q + 1)
                if q == 0:
                    pe.wait_ge(s_rel, 32)
                pe.wait_ge(s_x1, q + 1)
                pe.transpose(ps[0:D, 2, 0:LO], x1[0:LO, q % 2, :], ident[0:LO, 0:LO]).then_inc(s_x1ps, 1)
                pe.wait_ge(s_x1T, q + 1)
                for c in range(4):
                    if q >= 1:
                        pe.wait_ge(s_ysb, 4 * (q - 1) + c + 1)
                    pe.matmul(ps[0:LO, 3 + c, :], x1T[:, q % 2, 0:LO], rel[:, c * 512:(c + 1) * 512], start=True, stop=True).then_inc(s_y, 1)
                if q >= 1:
                    pe.wait_ge(s_selfsb, q)
                pe.matmul(ps[0:LO, 7, 0:D], x1T[:, q % 2, 0:LO], rel[:, R * D:(R + 1) * D], start=True, stop=True).then_inc(s_selfps, 1)

            m2 = pe.value_load(passes[0:1, 1:2], min_val=1, max_val=N)
            pe.wait_ge(s_selfsb, HI)
            pe.wait_ge(s_ysb, 4 * HI)
            pe.sem_inc(oh2_free, 2)
            with pe.Fori(0, m2) as v:
                with pe.Fori(0, NPAIR) as i:
                    for s in range(2):
                        pe.wait_ge(oh2_ready, v * NG + i * 2 + s + 1)
                        pe.wait_ge(msg_free, v * NG + i * 2 + s + 1)
                        pe.wait_ge(s_got[s], (v * NPAIR + i + 1) * (16 * J))
                        for j in range(J):
                            for h in range(Q2):
                                last = pe.matmul(ps[0:LO, 2 * s + h, 0:D], oh2[:, s, j, h * LO:(h + 1) * LO], got[:, s, j, :],
                                                 start=(j == 0), stop=(j == J - 1))
                        last.then_inc(msg_done, 1)
                        pe.wait_ge(msg_done, v * NG + i * 2 + s + 1)
                        pe.sem_inc(oh2_free, 1)

        @block.vector
        def _(dve):
            steps = [0]

            def step(ins):
                steps[0] += 1
                ins.then_inc(d_step, 1)
                dve.wait_ge(d_step, steps[0])

            def chunked(a, c):
                return a.rearrange("p (c e) -> p c e", c=C)[:, c, :]

            dve.wait_ge(s_dst, 48)
            step(dve.tensor_copy(dstF, raw[1]))
            dve.tensor_reduce(sm[:, 0:2], dstF.rearrange("p (c e) -> p c e", c=C), axis=AX.X, op=ALU.min)
            step(dve.tensor_reduce(sm2[:, 0:2], dstF.rearrange("p (c e) -> p c e", c=C), axis=AX.X, op=ALU.max))
            step(dve.tensor_scalar(sm2[:, 2:4], sm[:, 0:2], 1.0 / LO, 0.5 / LO - 0.5, ALU.mult, ALU.add))
            step(dve.tensor_scalar(sm[:, 2:4], sm2[:, 2:4], ROUND, -ROUND, ALU.add, ALU.add))
            step(dve.tensor_scalar(sm2[:, 4:6], sm[:, 2:4], float(LO), None, ALU.mult))
            step(dve.tensor_tensor(sm2[:, 2:4], sm2[:, 0:2], sm[:, 0:2], ALU.subtract))
            step(dve.tensor_tensor(sm2[:, 0:2], sm2[:, 0:2], sm2[:, 4:6], ALU.subtract))
            step(dve.tensor_reduce(sm[:, 4:5], sm2[:, 2:4], axis=AX.X, op=ALU.max))
            dve.tensor_reduce(sm[:, 5:6], sm2[:, 0:2], axis=AX.X, op=ALU.max).then_inc(s_keysF, 1)
            dve.wait_ge(s_src, 48)
            step(dve.tensor_copy(srcF, raw[0]))
            step(dve.tensor_scalar(keyF, srcF, 1.0 / LO, 0.5 / LO - 0.5, ALU.mult, ALU.add))
            step(dve.tensor_scalar(hiF, keyF, ROUND, -ROUND, ALU.add, ALU.add))
            dve.wait_ge(s_typ, 48)
            step(dve.tensor_copy(typF, raw[2]))
            step(dve.scalar_tensor_tensor(typF, srcF, float(R), typF, ALU.mult, ALU.add))
            step(dve.scalar_tensor_tensor(srcF, hiF, -float(LO), srcF, ALU.mult, ALU.add))
            dve.nop().then_inc(s_keysF, 1)
            for c in range(C):
                dve.tensor_scalar(chunked(key2F, c), chunked(dstF, c), sm2[:, 4 + c:5 + c], None, ALU.subtract)
                step(dve.tensor_scalar(chunked(keyF, c), chunked(dstF, c), sm[:, c:c + 1], None, ALU.subtract))
            dve.wait_ge(s_eid, 1)
            step(dve.scalar_tensor_tensor(keyF, keyF, float(HI), hiF, ALU.mult, ALU.add))
            step(dve.tensor_scalar(eid, eid, 0.0, FAR, ALU.is_ge, ALU.mult))
            dve.tensor_tensor(chunked(keyF, 1), chunked(keyF, 1), eid, ALU.add)
            step(dve.tensor_tensor(chunked(key2F, 1), chunked(key2F, 1), eid, ALU.add))
            dve.nop().then_inc(s_keysF, 1)
            dve.wait_ge(s_rowT, 1)
            dve.tensor_copy(tabl[0:1, 0:GP], ps[0:1, 0, 0:GP])
            dve.tensor_scalar(tabl[0:1, GP:2 * GP], ps[0:1, 0, GP:2 * GP], float(D), None, ALU.mult)
            step(dve.tensor_reduce(cnts[:], ps[0:1, 1, 0:2 * P].rearrange("p (k n) -> p k n", k=2), axis=AX.X, op=ALU.max))
            dve.tensor_scalar(cnts[0:1, 0:1], cnts[0:1, 0:1], 1.0 / W, 0.5 / W - 0.5, ALU.mult, ALU.add)
            step(dve.tensor_scalar(cnts[0:1, 1:2], cnts[0:1, 1:2], 1.0 / KW2, 0.5 / KW2 - 0.5, ALU.mult, ALU.add))
            step(dve.tensor_scalar(cnts[:], cnts[:], ROUND, -ROUND, ALU.add, ALU.add))
            step(dve.tensor_scalar(passes[:], cnts[:], 1.0, None, ALU.add))
            dve.nop().then_inc(s_rows, 1)
            for k, to in enumerate((los, rows, keys, key2)):
                for c in range(C):
                    dve.wait_ge(s_keyT, 2 * k + c + 1)
                    last = dve.tensor_copy(to[:, :, c * P:(c + 1) * P],
                                           ps[:, 2 + (2 * k + c) % 6, :].rearrange("p (j n) -> p j n", j=J))
                step(last)
                dve.nop().then_inc(s_keysb, 1)
            dve.wait_ge(s_relw, 16)
            dve.memset(inside(TAIL + 5, 4 * ND), 0.0).then_inc(s_zero, 1)

            m1 = dve.value_load(passes[0:1, 0:1], min_val=1, max_val=N)
            dve.wait_ge(s_const, 3)
            dve.wait_ge(s_zero, 3)
            
            dve.sem_inc(win_free, 2)
            with dve.Fori(0, m1) as v:
                def one_hots(g, s):
                    for j in range(J):
                        dve.tensor_scalar(ohl[:, s, j, :], iota_k[:, 0:P], los[:, j, bass.ds(g, 1)], None, ALU.is_equal)
                    for j in range(J):
                        last = dve.tensor_scalar(ohk[:, s, j, :], iota_k[:], keys[:, j, bass.ds(g, 1)], None, ALU.is_equal)
                    last.then_inc(oh_ready, 1)

                def add_window(g, s, done):
                    base = dve.value_load(tabl[0:1, bass.ds(g, 1)], min_val=0, max_val=N)
                    dve.wait_ge(win_done, done)
                    dve.wait_ge(win_free, done + 1)
                    a = adj[:, :, bass.ds(base, W)]
                    dve.tensor_tensor(a, a, ps[:, s, 0:KW].rearrange("p (n h) -> p h n", h=HI), ALU.add).then_inc(win_free, 1)

                one_hots(0, 0)
                with dve.Fori(0, NPAIR - 1) as i:
                    g = i * 2
                    one_hots(g + 1, 1)
                    add_window(g, 0, v * NG + g + 1)
                    one_hots(g + 2, 0)
                    add_window(g + 1, 1, v * NG + g + 2)
                one_hots(NG - 1, 1)
                add_window(NG - 2, 0, v * NG + NG - 1)
                add_window(NG - 1, 1, v * NG + NG)
                dve.tensor_scalar(keys, keys, -float(KW), None, ALU.add).then_inc(s_adjfree, 1)
                dve.tensor_scalar(tabl[0:1, 0:GP], tabl[0:1, 0:GP], float(W), float(N), ALU.add, ALU.min).then_inc(s_adjfree, 1)
                dve.wait_ge(s_adjfree, v * 2 + 2)
            dve.nop().then_inc(s_prop, 1)

            dve.wait_ge(s_deg, 1)
            dve.memset(deg[:], 1.0)
            dve.tensor_scalar(rind[0:LO, :], ps[0:LO, 2, 0:HI], 1.0, None, ALU.max)
            step(dve.memset(split1[:, :, :], 0.0))
            step(dve.tensor_scalar(deg[0:LO, :], ps[0:LO, 2, 0:HI], 1.0, None, ALU.add))
            step(dve.reciprocal(rind[0:LO, :], rind[0:LO, :]))
            step(dve.nop())
            dve.nop().then_inc(s_var, 1)
            dve.wait_ge(s_std, 1)
            step(dve.memset(split2, 0.0))
            step(dve.reciprocal(dinv[:], dinv[:]))
            step(dve.tensor_tensor(dinv2[:], dinv[:], dinv[:], ALU.mult))
            dve.wait_ge(s_xws, 7)
            step(dve.tensor_tensor(prop[0:LO], prop[0:LO], dinv[0:LO, :, None].to_broadcast([LO, HI, D]), ALU.mult))

            def three_parts(to, of, rest):
                step(dve.tensor_copy(to(0), of))
                step(dve.tensor_tensor(rest, of, to(0), ALU.subtract))
                step(dve.tensor_copy(to(1), rest))
                step(dve.tensor_tensor(to(2), rest, to(1), ALU.subtract))

            rest1 = u2[0:LO, 0:2 * HI * D].bitcast(fp32).rearrange("p (h d) -> p h d", h=HI)
            three_parts(lambda k: split1[0:LO, :, k * D:(k + 1) * D], prop[0:LO, :, :], rest1)
            dve.nop().then_inc(s_prop, 1)

            def hop_sum(q, n):
                dve.wait_ge(s_hop, n + 1)
                step(dve.tensor_reduce(tmp[0:LO, 0, :], ps[0:LO, n % 2, 0:3 * D].rearrange("p (k d) -> p d k", k=3), axis=AX.X, op=ALU.add))
                dve.nop().then_inc(s_hopfree, 1)
                step(dve.tensor_tensor(tmp[0:LO, 1, :], tmp[0:LO, 0, :], prop[0:LO, q, :], ALU.add))

            for q in range(HI):
                hop_sum(q, q)
                step(dve.tensor_scalar(prop[0:LO, q, :], tmp[0:LO, 1, :], dinv2[0:LO, q:q + 1], None, ALU.mult))
                three_parts(lambda k: split2[0:LO, q, k * D:(k + 1) * D], prop[0:LO, q, :], tmp[0:LO, 2, :])
                dve.nop().then_inc(s_split2, 1)
            dve.wait_ge(s_bias, 32)
            def self_part(q):
                step(dve.tensor_tensor(xs[0:LO, q, :], x1[0:LO, q % 2, :], biasvec[0:LO, :], ALU.add))
                dve.wait_ge(s_selfps, q + 1)
                dve.tensor_tensor(xs[0:LO, q, :], ps[0:LO, 7, 0:D], xs[0:LO, q, :], ALU.add).then_inc(s_selfsb, 1)

            for q in range(HI):
                hop_sum(q, HI + q)
                step(dve.scalar_tensor_tensor(tmp[0:LO, 0, :], tmp[0:LO, 1, :], dinv[0:LO, q:q + 1], bvec[0:LO, :], ALU.mult, ALU.add))
                step(dve.scalar_tensor_tensor(tmp[0:LO, 1, :], tmp[0:LO, 0, :], 0.0, xs[0:LO, q, :], ALU.max, ALU.add))
                step(dve.bn_stats(stats[0:LO, :], tmp[0:LO, 1, :]))
                dve.bn_aggr(mv[0:LO, :], stats[0:LO, :]).then_inc(s_var, 1)
                dve.wait_ge(s_std, q + 2)
                step(dve.reciprocal(rstd[0:LO, q % 2:q % 2 + 1], rstd[0:LO, q % 2:q % 2 + 1]))
                if q >= 2:
                    dve.wait_ge(s_x1ps, q - 1)
                dve.tensor_scalar(x1[0:LO, q % 2, :], tmp[0:LO, 1, :], mv[0:LO, 0:1], rstd[0:LO, q % 2:q % 2 + 1], ALU.subtract, ALU.mult).then_inc(s_x1, 1)
                dve.wait_ge(s_x1, q + 1)
                if q >= 1:
                    self_part(q - 1)
            self_part(HI - 1)

            m2 = dve.value_load(passes[0:1, 1:2], min_val=1, max_val=N)
            dve.memset(acc, 0.0).then_inc(s_accz, 1)
            dve.wait_ge(s_const, 4)
            dve.wait_ge(s_accz, 1)
            dve.sem_inc(msg_free, 2)
            with dve.Fori(0, m2) as v:
                def one_hots2(g, s, n):
                    dve.wait_ge(oh2_free, n)
                    dve.tensor_tensor(oh2[:, s, :, :], iota_2[:, None, :].to_broadcast([P, J, KW2]),
                                      key2[:, :, bass.ds(g, 1)].to_broadcast([P, J, KW2]), ALU.is_equal).then_inc(oh2_ready, 1)

                def add_message(g, s, done):
                    col = dve.value_load(tabl[0:1, bass.ds(g + GP, 1)], min_val=0, max_val=HI * D)
                    dve.wait_ge(msg_done, done)
                    dve.wait_ge(msg_free, done + 1)
                    a = acc[0:LO, bass.ds(col, Q2 * D)].rearrange("p (q d) -> p q d", q=Q2)
                    dve.tensor_tensor(a, a, ps[0:LO, 2 * s:2 * s + 2, 0:D], ALU.add).then_inc(msg_free, 1)

                one_hots2(0, 0, v * NG + 1)
                with dve.Fori(0, NPAIR - 1) as i:
                    g = i * 2
                    one_hots2(g + 1, 1, v * NG + g + 2)
                    add_message(g, 0, v * NG + g + 1)
                    one_hots2(g + 2, 0, v * NG + g + 3)
                    add_message(g + 1, 1, v * NG + g + 2)
                one_hots2(NG - 1, 1, v * NG + NG)
                add_message(NG - 2, 0, v * NG + NG - 1)
                add_message(NG - 1, 1, v * NG + NG)
                dve.tensor_scalar(key2[:], key2[:], -float(KW2), None, ALU.add).then_inc(s_accz, 1)
                dve.tensor_scalar(tabl[0:1, GP:2 * GP], tabl[0:1, GP:2 * GP], float(Q2 * D), float(HI * D), ALU.add, ALU.min).then_inc(s_accz, 1)
                dve.wait_ge(s_accz, v * 2 + 3)

            a3 = acc[0:LO, 0:HI * D].rearrange("p (h d) -> p h d", h=HI)
            yv, y2v = y[0:LO], y2[0:LO]
            step(dve.tensor_tensor(yv, a3, rind[0:LO, :, None].to_broadcast([LO, HI, D]), ALU.mult))
            step(dve.tensor_tensor(yv, yv, xs[0:LO], ALU.add))
            step(dve.tensor_reduce(mean[0:LO, :], yv, axis=AX.X, op=ALU.add))
            step(dve.tensor_scalar(mean[0:LO, :], mean[0:LO, :], 1.0 / D, None, ALU.mult))
            step(dve.tensor_tensor(yv, yv, mean[0:LO, :, None].to_broadcast([LO, HI, D]), ALU.subtract))
            step(dve.tensor_tensor(y2v, yv, yv, ALU.mult))
            step(dve.tensor_reduce(var[0:LO, :], y2v, axis=AX.X, op=ALU.add))
            dve.nop().then_inc(s_fv, 1)
            dve.wait_ge(s_fs, 1)
            step(dve.reciprocal(var[0:LO, :], var[0:LO, :]))
            step(dve.tensor_tensor(yv, yv, var[0:LO, :, None].to_broadcast([LO, HI, D]), ALU.mult))
            dve.nop().then_inc(s_fin, 1)


_INS = ['x', 'src', 'dst', 'edge_type_32', 'L0_gnn_W', 'L0_gnn_b', 'L1_gnn_basis', 'L1_gnn_coeff', 'L1_gnn_self_weight', 'L1_gnn_bias']


def kernel(**inputs):
    import numpy as _np
    import concourse.bacc as _bacc
    from concourse import mybir as _mybir
    from concourse.bass_utils import run_bass_kernel_spmd as _run

    nc = _bacc.Bacc("TRN2", target_bir_lowering=False, num_devices=1)
    arrays, args = {}, []
    for name in _INS:
        a = _np.ascontiguousarray(inputs[name])
        arrays[f"in_{name}"] = a
        args.append(nc.dram_tensor(f"in_{name}", a.shape, _mybir.dt.from_np(a.dtype), kind="ExternalInput").ap())
    out = nc.dram_tensor("out", (N, D), _mybir.dt.float32, kind="ExternalOutput").ap()
    build(nc, *args, out)
    r = _run(nc, [arrays], core_ids=[0])
    return r.results[0]["out"]
```

```python
from contextlib import ExitStack

import concourse.bass as bass
from concourse import mybir

N, D, E, R, B = 3125, 64, 103125, 32, 30
LO, HI = 125, 25
P = 128
J = 4
GE = J * P
NG = -(-E // GE)
C = -(-NG // P)
GP = C * P
NPAIR = NG // 2
NQUAD = NG // 4
ONE = LO
W = 18
KW = W * HI
ND = N + 19
Q2 = 2
KW2 = Q2 * LO
ROUND = 12582912.0
FAR = -1048576.0
EPS = 1e-5
KEYS, LOS, KEY2, ROWS = range(4)


def build(nc, x, src, dst, typ, w, b, basis, coeff, selfw, bias, out):
    fp32, i32 = mybir.dt.float32, mybir.dt.int32
    bf16, fp16 = mybir.dt.bfloat16, mybir.dt.float16
    ALU, ACT, AX = mybir.AluOpType, mybir.ActivationFunctionType, mybir.AxisListType
    ctx = ExitStack()
    with ctx:
        def sb(name, shape, dt):
            return ctx.enter_context(nc.sbuf_tensor(name, shape, dt))

        def sem(name):
            return ctx.enter_context(nc.semaphore(name))

        rel_dram = nc.dram_tensor("rel_dram", (R, D, D), fp32, kind="Internal").ap()
        count_dram = nc.dram_tensor("count_dram", (HI, N), bf16, kind="Internal").ap()
        deg_dram = nc.dram_tensor("deg_dram", (N,), fp32, kind="Internal").ap()
        table = nc.dram_tensor("table", (N * R, D), fp32, kind="Internal").ap()

        adj = sb("adj", [P, HI, ND], bf16)
        adj_flat = adj[:, :, :].rearrange("p h n -> p (h n)")

        def inside(first_hi, words, dt=fp32):
            start = first_hi * ND
            return adj_flat[:, start:start + 2 * words].bitcast(dt)

        TM = C * GE
        TAIL = 12
        def tm(n, dt=fp32):
            start = 18 * ND + n * 2 * TM
            return adj_flat[:, start:start + 2 * TM].bitcast(dt)
        raw = [tm(n, i32) for n in range(3)]
        srcF, dstF, typF, hiF, keyF, key2F = (tm(n) for n in range(3, 9))
        eid = adj_flat[:, 18 * ND + 9 * 2 * TM:18 * ND + 9 * 2 * TM + 2 * GE].bitcast(fp32)
        basis_sb = inside(12, D * D)
        rel_sb = inside(15, D * D)
        oh2 = inside(0, 2 * J * KW2).rearrange("p (s j k) -> p s j k", s=2, j=J)
        got = inside(13, 4 * J * D).rearrange("p (s j d) -> p s j d", s=4, j=J)
        acc = inside(4, (HI + Q2) * D)
        y = inside(7, HI * D).rearrange("p (h d) -> p h d", h=HI)
        iota_2 = inside(9, KW2)
        y2 = inside(10, HI * D).rearrange("p (h d) -> p h d", h=HI)

        split1 = sb("split1", [P, HI, 3 * D], bf16)
        rel = split1[:, :, :].rearrange("p h d -> p (h d)")[:, 0:2 * (R + 1) * D].bitcast(fp32)
        xT = split1[0:D, :, :].rearrange("p h d -> p (h d)")[:, 0:2 * J * P * 2].bitcast(fp32).rearrange("p (s n) -> p s n", s=2)
        u1 = sb("u1", [P, HI * 3 * D], bf16)
        split2 = u1[:, :].rearrange("p (h d) -> p h d", h=HI)
        keys = u1[:, 0:2 * J * GP].bitcast(fp32).rearrange("p (j g) -> p j g", j=J)
        los = u1[:, 2 * J * GP:4 * J * GP].bitcast(fp32).rearrange("p (j g) -> p j g", j=J)
        key2 = sb("key2", [P, J, GP], fp32)
        rows = sb("rows", [P, J, GP], fp32)
        prop = sb("prop", [P, HI, D], fp32)
        xs = sb("xs", [P, HI, D], fp32)
        u2 = sb("u2", [P, 2 * J * (KW + P)], bf16)
        ohk = u2[:, 0:2 * J * KW].rearrange("p (s j k) -> p s j k", s=2, j=J)
        ohl = u2[:, 2 * J * KW:].rearrange("p (s j k) -> p s j k", s=2, j=J)
        stage = u2[:, 0:4 * 2 * 512].bitcast(fp32).rearrange("p (s n) -> p s n", s=4)
        iota_k = sb("iota_k", [P, KW], fp16)
        ident = sb("ident", [P, P], fp32)
        bvec = sb("bvec", [P, D], fp32)
        biasvec = sb("biasvec", [P, D], fp32)
        head = u1[:, 0:2 * (2 * D + B + R)].bitcast(fp32)
        wt, wsb = head[0:D, 0:D], head[0:D, D:2 * D]
        cfsb, cft = head[0:R, 2 * D:2 * D + B], head[0:B, 2 * D + B:]
        sm = sb("sm", [P, 6], fp32)
        sm2 = sb("sm2", [P, 6], fp32)
        tabl = sb("tabl", [D, GP], i32)
        bases, columns = tabl[0:1, :], tabl[32:33, :]
        cnts = sb("cnts", [1, 2], fp32)
        passes = sb("passes", [1, 2], i32)
        dinv = sb("dinv", [P, HI], fp32)
        dinv2 = sb("dinv2", [P, HI], fp32)
        rind = sb("rind", [P, HI], fp32)
        deg = sb("deg", [P, HI], fp32)
        u3 = sb("u3", [P, 7 * D], fp32)
        tmp = u3[:, 0:3 * D].rearrange("p (n d) -> p n d", n=3)
        x1 = u3[:, 3 * D:].rearrange("p (s t d) -> p s t d", s=2, t=2)
        away = u3[:, 0:J * LO // 2].bitcast(fp16).rearrange("p (j k) -> p j k", j=J)
        x1T = u2[:, 4 * 2 * 512:4 * 2 * 512 + 4 * P].bitcast(fp32).rearrange("p (s n) -> p s n", s=2)
        stats = sb("stats", [P, 6], fp32)
        mv = sb("mv", [P, 2], fp32)
        rstd = sb("rstd", [P, 2], fp32)
        idx = sb("idx", [P, 4, J], i32)
        count_part = split1[:, :, 0:HI]
        degp = u2[:, 0:2 * HI].bitcast(fp32)
        degh = u2[0:HI, 2 * HI:2 * HI + 2 * LO].bitcast(fp32)
        mean = inside(6, 2 * HI)[:, 0:HI]
        var = inside(6, 2 * HI)[:, HI:]
        epsv = sb("epsv", [P, 1], fp32)
        ps = ctx.enter_context(nc.psum_tensor("ps", [P, 8, 512], fp32))

        s_src, s_dst, s_typ = sem("s_src"), sem("s_dst"), sem("s_typ")
        s_pad = sem("s_pad")
        s_x, s_small, s_basis, s_self, s_rel, s_relw, s_bias = (sem(n) for n in ("s_x", "s_small", "s_basis", "s_self", "s_rel", "s_relw", "s_bias"))
        s_c0, s_ident, s_const, s_eid = (sem(n) for n in ("s_c0", "s_ident", "s_const", "s_eid"))
        s_head, s_wt, s_relps, s_relsb, s_xT, s_xTs, s_xw, s_xws = (sem(n) for n in ("s_head", "s_wt", "s_relps", "s_relsb", "s_xT", "s_xTs", "s_xw", "s_xws"))
        d_step = sem("d_step")
        s_keysF, s_keyT, s_keysb, s_rowT, s_rows, s_zero = (sem(n) for n in ("s_keysF", "s_keyT", "s_keysb", "s_rowT", "s_rows", "s_zero"))
        key_ready, win_done, win_free = (sem(n) for n in ("key_ready", "win_done", "win_free"))
        s_deg, s_prop, s_hop, s_hopfree, s_split2, s_var, s_std = (sem(n) for n in ("s_deg", "s_prop", "s_hop", "s_hopfree", "s_split2", "s_var", "s_std"))
        s_x1, s_x1ps, s_x1T, s_y, s_ysb, s_selfps, s_selfsb = (sem(n) for n in ("s_x1", "s_x1ps", "s_x1T", "s_y", "s_ysb", "s_selfps", "s_selfsb"))
        s_yout = [sem(f"s_yout{i}") for i in range(4)]
        s_adjfree, s_accz, slot_taken = sem("s_adjfree"), sem("s_accz"), sem("slot_taken")
        oh2_ready, msg_done, msg_free, idx_ready = (sem(n) for n in ("oh2_ready", "msg_done", "msg_free", "idx_ready"))
        s_got = [sem(f"s_got{i}") for i in range(4)]
        s_cnt, s_degp, lo_ready, s_away, s_lo1 = (sem(n) for n in ("s_cnt", "s_degp", "lo_ready", "s_away", "s_lo1"))
        s_fv, s_fs, s_fin, s_out = sem("s_fv"), sem("s_fs"), sem("s_fin"), sem("s_out")

        block = ctx.enter_context(nc.Block())
        FULL = E // GE
        TOP = FULL - P
        LAST = E - FULL * GE

        @block.sync
        def _(sp):
            sp.wait_ge(s_pad, 3)
            for a, r, s in ((dst, raw[1], s_dst), (src, raw[0], s_src), (typ, raw[2], s_typ)):
                v = r.rearrange("p (c e) -> p c e", c=C)
                sp.dma_start(v[:, 0, :], a[0:P * GE].rearrange("(p e) -> p e", p=P)).then_inc(s, 16)
                sp.dma_start(v[0:TOP, 1, :], a[P * GE:FULL * GE].rearrange("(p e) -> p e", e=GE)).then_inc(s, 16)
                sp.dma_start(v[TOP:TOP + 1, 1, 0:LAST], a[FULL * GE:E].rearrange("(p e) -> p e", p=1)).then_inc(s, 16)
            sp.wait_ge(s_relsb, 8)
            sp.dma_start(rel_dram.rearrange("r i o -> r (i o)"), rel_sb[0:R, :]).then_inc(s_relw, 16)
            sp.wait_ge(s_relw, 16)
            sp.wait_ge(s_prop, 1)
            sp.dma_start(count_dram[None, :, :], adj[ONE:ONE + 1, :, 0:N]).then_inc(s_cnt, 16)
            sp.wait_ge(s_cnt, 16)
            sp.dma_start(count_part[0:LO], count_dram.rearrange("h (p m) -> p h m", p=LO)).then_inc(s_cnt, 16)
            sp.wait_ge(s_degp, 1)
            sp.dma_start(deg_dram.rearrange("(p m) -> p m", p=LO), degp[0:LO, :]).then_inc(s_cnt, 16)
            sp.wait_ge(s_cnt, 48)
            sp.dma_start(degh, deg_dram.rearrange("(h l) -> h l", l=LO)).then_inc(s_cnt, 16)
            sp.wait_ge(s_hop, HI)
            for half in (rel[0:D], rel[D:2 * D]):
                sp.dma_start(half[:, 0:R * D].rearrange("i (r o) -> i r o", r=R), rel_dram.rearrange("r i o -> i r o")).then_inc(s_rel, 16)
                sp.dma_start(half[:, R * D:(R + 1) * D], selfw).then_inc(s_rel, 16)
            tv = table.rearrange("(n r) d -> n (r d)", r=R)
            for q in range(HI):
                for c in range(4):
                    sp.wait_ge(s_ysb, 4 * q + c + 1)
                    sp.dma_start(tv[q * LO:(q + 1) * LO, c * 512:(c + 1) * 512], stage[0:LO, c, :]).then_inc(s_yout[c], 16)
            sp.wait_ge(s_fin, 1)
            sp.dma_start(out.rearrange("(h l) d -> l h d", l=LO), y[0:LO, :, :]).then_inc(s_out, 16)
            sp.wait_ge(s_out, 16)

        @block.gpsimd
        def _(pool):
            pool.memset(raw[0], 0).then_inc(s_pad, 1)
            pool.memset(raw[1], N - 1).then_inc(s_pad, 1)
            pool.memset(raw[2], 0).then_inc(s_pad, 1)
            pool.memset(ident[:], 0.0).then_inc(s_c0, 1)
            pool.wait_ge(s_c0, 1)
            pool.affine_select(out=ident[:], in_=ident[:], compare_op=ALU.not_equal, fill=1.0, base=0,
                               pattern=[[-1, P]], channel_multiplier=1).then_inc(s_ident, 1)
            pool.iota(eid, [[1, GE]], base=P * GE - E, channel_multiplier=GE,
                      allow_small_or_imprecise_dtypes=True).then_inc(s_eid, 1)
            pool.iota(iota_k[:], [[1, KW]], base=0, channel_multiplier=0, allow_small_or_imprecise_dtypes=True).then_inc(s_const, 1)
            pool.memset(ohl, 0.0).then_inc(s_c0, 1)
            pool.wait_ge(s_c0, 2)
            pool.memset(ohl[:, :, :, ONE:ONE + 1], 1.0).then_inc(s_lo1, 1)
            pool.nop().then_inc(s_const, 1)
            pool.memset(epsv[:], EPS).then_inc(s_const, 1)
            pool.memset(inside(0, TAIL * ND // 2), 0.0).then_inc(s_zero, 1)
            pool.wait_ge(s_keyT, 8)
            pool.wait_ge(s_relw, 16)
            pool.memset(inside(TAIL, 5 * ND // 2), 0.0).then_inc(s_zero, 1)

            pool.wait_ge(s_rows, 1)
            m2 = pool.value_load(passes[0:1, 1:2], min_val=1, max_val=N)
            for c in range(4):
                pool.wait_ge(s_yout[c], 16 * HI)
            pool.iota(iota_2, [[1, KW2]], base=0, channel_multiplier=0, allow_small_or_imprecise_dtypes=True).then_inc(s_const, 1)
            with pool.Fori(0, m2) as v:
                def gather(g, s):
                    pool.wait_ge(idx_ready, v * NG + g + 1)
                    pool.sem_inc(slot_taken, 1)
                    for j in range(J):
                        pool.indirect_dma_start(got[:, s, j, :], None, table,
                                                bass.IndirectOffsetOnAxis(ap=idx[:, s, j:j + 1], axis=0)).then_inc(s_got[s], 16)

                with pool.Fori(0, NQUAD) as i:
                    for s in range(4):
                        gather(i * 4 + s, s)
                for s in range(2):
                    gather(NQUAD * 4 + s, s)

        @block.scalar
        def _(act):
            act.dma_start(wsb, w).then_inc(s_small, 16)
            act.dma_start(cfsb, coeff).then_inc(s_small, 16)
            act.dma_start(xs[0:LO, :, :], x.rearrange("(h l) d -> l h d", l=LO)).then_inc(s_x, 16)
            act.dma_start(basis_sb[0:B, :], basis.rearrange("b i o -> b (i o)")).then_inc(s_basis, 16)
            act.dma_start(bvec[:], b[None, :].to_broadcast([P, D])).then_inc(s_bias, 16)
            act.dma_start(biasvec[:], bias[None, :].to_broadcast([P, D])).then_inc(s_bias, 16)
            act.wait_ge(s_head, 2)
            act.copy(wt, ps[0:D, 0, 0:D]).then_inc(s_wt, 1)
            act.copy(cft, ps[0:B, 1, 0:R]).then_inc(s_wt, 1)
            for k in range(8):
                act.wait_ge(s_relps, k + 1)
                act.copy(rel_sb[0:R, k * 512:(k + 1) * 512], ps[0:R, 2 + k % 2, :]).then_inc(s_relsb, 1)
            for k in range(7):
                n = min(4, HI - 4 * k)
                act.wait_ge(s_xT, k + 1)
                if k >= 2:
                    act.wait_ge(s_xw, k - 1)
                act.copy(xT[:, k % 2, 0:n * LO], ps[0:D, 4 + k % 2, 0:n * LO]).then_inc(s_xTs, 1)
                act.wait_ge(s_xw, k + 1)
                act.copy(prop[0:LO, 4 * k:4 * k + n, :], ps[0:LO, 6 + k % 2, 0:n * D].rearrange("p (n d) -> p n d", n=n)).then_inc(s_xws, 1)
            act.wait_ge(s_rows, 1)
            m1 = act.value_load(passes[0:1, 0:1], min_val=1, max_val=N)
            act.wait_ge(s_keysb, 4)
            act.wait_ge(s_const, 3)
            act.wait_ge(s_lo1, 1)
            act.sem_inc(lo_ready, 1)
            with act.Fori(0, m1) as v:
                with act.Fori(0, NPAIR) as i:
                    for s in range(2):
                        n = v * NG + i * 2 + s
                        act.wait_ge(lo_ready, n + 1)
                        for j in range(J):
                            last = act.activation(away[:, j, :], iota_k[:, 0:LO], ACT.Abs, bias=los[:, j, bass.ds(i * 2 + s, 1)])
                        last.then_inc(s_away, 1)
                        act.wait_ge(s_away, n + 1)
                        act.wait_ge(win_done, n + 1)
                        act.activation(ohl[:, s, :, 0:LO], away, ACT.Relu, scale=-1.0, bias=1.0).then_inc(lo_ready, 1)
            act.wait_ge(s_var, 1)
            act.wait_ge(s_const, 3)
            act.activation(dinv[:], deg[:], ACT.Sqrt).then_inc(s_std, 1)
            for q in range(HI):
                act.wait_ge(s_var, q + 2)
                act.activation(rstd[0:LO, q % 2:q % 2 + 1], mv[0:LO, 1:2], ACT.Sqrt, bias=epsv[0:LO, :]).then_inc(s_std, 1)
                act.wait_ge(s_x1ps, q + 1)
                act.copy(x1T[:, q % 2, 0:LO], ps[:, 2, 0:LO]).then_inc(s_x1T, 1)
                for c in range(4):
                    act.wait_ge(s_y, 4 * q + c + 1)
                    if q >= 1:
                        act.wait_ge(s_yout[c], 16 * q)
                    act.copy(stage[0:LO, c, :], ps[0:LO, 3 + c, :]).then_inc(s_ysb, 1)
            act.wait_ge(s_rows, 1)
            m2 = act.value_load(passes[0:1, 1:2], min_val=1, max_val=N)
            with act.Fori(0, m2) as v:
                def number(g, s):
                    act.wait_ge(msg_done, v * NG + g + 1)
                    act.copy(idx[:, s, :], rows[:, :, bass.ds(g, 1)].rearrange("p j o -> p (j o)")).then_inc(idx_ready, 1)

                with act.Fori(0, NQUAD) as i:
                    for s in range(4):
                        number(i * 4 + s, s)
                for s in range(2):
                    number(NQUAD * 4 + s, s)
            act.wait_ge(s_fv, 1)
            act.activation(var[0:LO, :], var[0:LO, :], ACT.Sqrt, bias=epsv[0:LO, :], scale=1.0 / D).then_inc(s_fs, 1)

        @block.tensor
        def _(pe):
            pe.wait_ge(s_ident, 1)
            pe.wait_ge(s_small, 32)
            pe.transpose(ps[0:D, 0, 0:D], wsb, ident[0:D, 0:D]).then_inc(s_head, 1)
            pe.transpose(ps[0:B, 1, 0:R], cfsb, ident[0:R, 0:R]).then_inc(s_head, 1)
            pe.wait_ge(s_wt, 2)
            pe.wait_ge(s_basis, 16)
            for k in range(8):
                if k >= 2:
                    pe.wait_ge(s_relsb, k - 1)
                pe.matmul(ps[0:R, 2 + k % 2, :], cft, basis_sb[0:B, k * 512:(k + 1) * 512], start=True, stop=True).then_inc(s_relps, 1)
            pe.wait_ge(s_x, 16)

            def x_transpose(k):
                n = min(4, HI - 4 * k)
                if k >= 2:
                    pe.wait_ge(s_xTs, k - 1)
                for m in range(n):
                    last = pe.transpose(ps[0:D, 4 + k % 2, m * LO:(m + 1) * LO], xs[0:LO, 4 * k + m, :], ident[0:LO, 0:LO])
                last.then_inc(s_xT, 1)

            x_transpose(0)
            for k in range(7):
                if k < 6:
                    x_transpose(k + 1)
                n = min(4, HI - 4 * k)
                pe.wait_ge(s_xTs, k + 1)
                if k >= 2:
                    pe.wait_ge(s_xws, k - 1)
                for m in range(n):
                    last = pe.matmul(ps[0:LO, 6 + k % 2, m * D:(m + 1) * D], xT[:, k % 2, m * LO:(m + 1) * LO], wt, start=True, stop=True)
                last.then_inc(s_xw, 1)
            pe.wait_ge(s_xws, 7)
            pe.wait_ge(s_keysF, 1)
            for k in range(6):
                last = pe.transpose(ps[0:1, k // 4, (k % 4) * P:(k % 4 + 1) * P], sm[:, k:k + 1], ident[:])
            last.then_inc(s_rowT, 1)
            for k, (arr, need) in enumerate(((srcF, 2), (typF, 2), (keyF, 3), (key2F, 3))):
                pe.wait_ge(s_keysF, need)
                v = arr.rearrange("p (c j e) -> p c j e", c=C, j=J)
                for c in range(C):
                    t = 2 + (2 * k + c) % 6
                    if 2 * k + c >= 6:
                        pe.wait_ge(s_keysb, 1)
                    for j in range(J):
                        last = pe.transpose(ps[:, t, j * P:(j + 1) * P], v[:, c, j, :], ident[:])
                    last.then_inc(s_keyT, 1)

            pe.wait_ge(s_rows, 1)
            m1 = pe.value_load(passes[0:1, 0:1], min_val=1, max_val=N)
            pe.wait_ge(s_keysb, 4)
            pe.sem_inc(win_done, 2)
            with pe.Fori(0, m1) as v:
                with pe.Fori(0, NPAIR) as i:
                    for s in range(2):
                        pe.wait_ge(lo_ready, v * NG + i * 2 + s + 2)
                        pe.wait_ge(key_ready, v * NG + i * 2 + s + 1)
                        pe.wait_ge(win_free, v * NG + i * 2 + s + 1)
                        for j in range(J):
                            last = pe.matmul(ps[:, s, 0:KW], ohl[:, s, j, :], ohk[:, s, j, :], start=(j == 0), stop=(j == J - 1))
                        last.then_inc(win_done, 1)

            pe.wait_ge(s_cnt, 64)
            pe.transpose(ps[0:LO, 2, 0:HI], degh, ident[0:HI, 0:HI]).then_inc(s_deg, 1)

            def hop(q, parts, n):
                if n >= 2:
                    pe.wait_ge(s_hopfree, n - 1)
                for h in range(HI):
                    last = pe.matmul(ps[0:LO, n % 2, 0:3 * D], adj[:, h, q * LO:(q + 1) * LO], parts[:, h, :], start=(h == 0), stop=(h == HI - 1))
                last.then_inc(s_hop, 1)

            pe.wait_ge(s_prop, 2)
            for q in range(HI):
                hop(q, split1, q)
            pe.wait_ge(s_split2, HI)
            hop(0, split2, HI)
            for q in range(HI):
                if q < HI - 1:
                    hop(q + 1, split2, HI + q + 1)
                if q == 0:
                    pe.wait_ge(s_rel, 64)
                pe.wait_ge(s_x1, q + 1)
                pe.transpose(ps[:, 2, 0:LO], x1[0:LO, q % 2, :, :].rearrange("p t d -> p (t d)"), ident[0:LO, 0:LO]).then_inc(s_x1ps, 1)
                pe.wait_ge(s_x1T, q + 1)
                for c in range(4):
                    if q >= 1:
                        pe.wait_ge(s_ysb, 4 * (q - 1) + c + 1)
                    a = D * (c % 2)
                    pe.matmul(ps[0:LO, 3 + c, :], x1T[a:a + D, q % 2, 0:LO], rel[a:a + D, c * 512:(c + 1) * 512], start=True, stop=True).then_inc(s_y, 1)
                if q >= 1:
                    pe.wait_ge(s_selfsb, q)
                pe.matmul(ps[0:LO, 7, 0:D], x1T[0:D, q % 2, 0:LO], rel[0:D, R * D:(R + 1) * D], start=True, stop=True).then_inc(s_selfps, 1)

            m2 = pe.value_load(passes[0:1, 1:2], min_val=1, max_val=N)
            pe.wait_ge(s_selfsb, HI)
            pe.wait_ge(s_ysb, 4 * HI)
            pe.sem_inc(msg_done, 4)
            with pe.Fori(0, m2) as v:
                def add_up(g, s, nth):
                    o = s % 2
                    pe.wait_ge(oh2_ready, v * NG + g + 1)
                    pe.wait_ge(msg_free, v * NG + g + 1)
                    pe.wait_ge(s_got[s], nth * (16 * J))
                    for j in range(J):
                        for h in range(Q2):
                            last = pe.matmul(ps[0:LO, 2 * o + h, 0:D], oh2[:, o, j, h * LO:(h + 1) * LO], got[:, s, j, :],
                                             start=(j == 0), stop=(j == J - 1))
                    last.then_inc(msg_done, 1)

                with pe.Fori(0, NQUAD) as i:
                    for s in range(4):
                        add_up(i * 4 + s, s, v * (NQUAD + (s < 2)) + i + 1)
                for s in range(2):
                    add_up(NQUAD * 4 + s, s, v * (NQUAD + 1) + NQUAD + 1)

        @block.vector
        def _(dve):
            steps = [0]

            def step(ins):
                steps[0] += 1
                ins.then_inc(d_step, 1)
                dve.wait_ge(d_step, steps[0])

            def chunked(a, c):
                return a.rearrange("p (c e) -> p c e", c=C)[:, c, :]

            dve.wait_ge(s_dst, 48)
            step(dve.tensor_copy(dstF, raw[1]))
            dve.tensor_reduce(sm[:, 0:2], dstF.rearrange("p (c e) -> p c e", c=C), axis=AX.X, op=ALU.min)
            step(dve.tensor_reduce(sm2[:, 0:2], dstF.rearrange("p (c e) -> p c e", c=C), axis=AX.X, op=ALU.max))
            step(dve.tensor_scalar(sm2[:, 2:4], sm[:, 0:2], 1.0 / LO, 0.5 / LO - 0.5, ALU.mult, ALU.add))
            step(dve.tensor_scalar(sm[:, 2:4], sm2[:, 2:4], ROUND, -ROUND, ALU.add, ALU.add))
            step(dve.tensor_scalar(sm2[:, 4:6], sm[:, 2:4], float(LO), None, ALU.mult))
            step(dve.tensor_tensor(sm2[:, 2:4], sm2[:, 0:2], sm[:, 0:2], ALU.subtract))
            step(dve.tensor_tensor(sm2[:, 0:2], sm2[:, 0:2], sm2[:, 4:6], ALU.subtract))
            step(dve.tensor_reduce(sm[:, 4:5], sm2[:, 2:4], axis=AX.X, op=ALU.max))
            dve.tensor_reduce(sm[:, 5:6], sm2[:, 0:2], axis=AX.X, op=ALU.max).then_inc(s_keysF, 1)
            dve.wait_ge(s_src, 48)
            step(dve.tensor_copy(srcF, raw[0]))
            step(dve.tensor_scalar(keyF, srcF, 1.0 / LO, 0.5 / LO - 0.5, ALU.mult, ALU.add))
            step(dve.tensor_scalar(hiF, keyF, ROUND, -ROUND, ALU.add, ALU.add))
            dve.wait_ge(s_typ, 48)
            step(dve.tensor_copy(typF, raw[2]))
            step(dve.scalar_tensor_tensor(typF, srcF, float(R), typF, ALU.mult, ALU.add))
            step(dve.scalar_tensor_tensor(srcF, hiF, float(LO), srcF, ALU.mult, ALU.subtract))
            dve.nop().then_inc(s_keysF, 1)
            for c in range(C):
                dve.tensor_scalar(chunked(key2F, c), chunked(dstF, c), sm2[:, 4 + c:5 + c], None, ALU.subtract)
                step(dve.tensor_scalar(chunked(keyF, c), chunked(dstF, c), sm[:, c:c + 1], None, ALU.subtract))
            dve.wait_ge(s_eid, 1)
            step(dve.scalar_tensor_tensor(keyF, keyF, float(HI), hiF, ALU.mult, ALU.add))
            step(dve.tensor_scalar(eid, eid, 0.0, FAR, ALU.is_ge, ALU.mult))
            dve.tensor_tensor(chunked(keyF, 1), chunked(keyF, 1), eid, ALU.add)
            step(dve.tensor_tensor(chunked(key2F, 1), chunked(key2F, 1), eid, ALU.add))
            dve.nop().then_inc(s_keysF, 1)
            dve.wait_ge(s_rowT, 1)
            dve.tensor_copy(bases, ps[0:1, 0, 0:GP])
            dve.tensor_scalar(columns, ps[0:1, 0, GP:2 * GP], float(D), None, ALU.mult)
            step(dve.tensor_reduce(cnts[:], ps[0:1, 1, 0:2 * P].rearrange("p (k n) -> p k n", k=2), axis=AX.X, op=ALU.max))
            dve.tensor_scalar(cnts[0:1, 0:1], cnts[0:1, 0:1], 1.0 / W, 0.5 / W - 0.5, ALU.mult, ALU.add)
            step(dve.tensor_scalar(cnts[0:1, 1:2], cnts[0:1, 1:2], 1.0 / KW2, 0.5 / KW2 - 0.5, ALU.mult, ALU.add))
            step(dve.tensor_scalar(cnts[:], cnts[:], ROUND, -ROUND, ALU.add, ALU.add))
            step(dve.tensor_scalar(passes[:], cnts[:], 1.0, None, ALU.add))
            dve.nop().then_inc(s_rows, 1)
            for k, to in enumerate((los, rows, keys, key2)):
                for c in range(C):
                    dve.wait_ge(s_keyT, 2 * k + c + 1)
                    last = dve.tensor_copy(to[:, :, c * P:(c + 1) * P],
                                           ps[:, 2 + (2 * k + c) % 6, :].rearrange("p (j n) -> p j n", j=J))
                step(last)
                dve.nop().then_inc(s_keysb, 1)
            dve.wait_ge(s_relw, 16)
            dve.memset(inside(TAIL + 5, 4 * ND), 0.0).then_inc(s_zero, 1)

            m1 = dve.value_load(passes[0:1, 0:1], min_val=1, max_val=N)
            dve.wait_ge(s_const, 3)
            dve.wait_ge(s_zero, 3)
            
            dve.sem_inc(win_free, 2)
            with dve.Fori(0, m1) as v:
                def one_hots(g, s):
                    for j in range(J):
                        last = dve.tensor_scalar(ohk[:, s, j, :], iota_k[:], keys[:, j, bass.ds(g, 1)], None, ALU.is_equal)
                    last.then_inc(key_ready, 1)

                def add_window(g, s, done):
                    base = dve.value_load(bases[0:1, bass.ds(g, 1)], min_val=0, max_val=N)
                    dve.wait_ge(win_done, done + 2)
                    dve.wait_ge(win_free, done + 1)
                    a = adj[:, :, bass.ds(base, W)]
                    dve.tensor_tensor(a, a, ps[:, s, 0:KW].rearrange("p (n h) -> p h n", h=HI), ALU.add).then_inc(win_free, 1)

                one_hots(0, 0)
                with dve.Fori(0, NPAIR - 1) as i:
                    g = i * 2
                    one_hots(g + 1, 1)
                    add_window(g, 0, v * NG + g + 1)
                    one_hots(g + 2, 0)
                    add_window(g + 1, 1, v * NG + g + 2)
                one_hots(NG - 1, 1)
                add_window(NG - 2, 0, v * NG + NG - 1)
                add_window(NG - 1, 1, v * NG + NG)
                dve.tensor_scalar(keys, keys, -float(KW), None, ALU.add).then_inc(s_adjfree, 1)
                dve.tensor_scalar(bases, bases, float(W), float(N), ALU.add, ALU.min).then_inc(s_adjfree, 1)
                dve.wait_ge(s_adjfree, v * 2 + 2)
            step(dve.memset(deg[:], 1.0))
            dve.nop().then_inc(s_prop, 1)

            dve.wait_ge(s_cnt, 32)
            step(dve.tensor_reduce(degp[0:LO, :], count_part[0:LO].rearrange("p h m -> p m h"), axis=AX.X, op=ALU.add))
            dve.nop().then_inc(s_degp, 1)
            step(dve.memset(split1[:, :, :], 0.0))
            dve.wait_ge(s_deg, 1)
            step(dve.tensor_scalar(rind[0:LO, :], ps[0:LO, 2, 0:HI], 1.0, None, ALU.max))
            step(dve.tensor_scalar(deg[0:LO, :], ps[0:LO, 2, 0:HI], 1.0, None, ALU.add))
            step(dve.reciprocal(rind[0:LO, :], rind[0:LO, :]))
            step(dve.nop())
            dve.nop().then_inc(s_var, 1)
            dve.wait_ge(s_std, 1)
            step(dve.memset(split2, 0.0))
            step(dve.reciprocal(dinv[:], dinv[:]))
            step(dve.tensor_tensor(dinv2[:], dinv[:], dinv[:], ALU.mult))
            dve.wait_ge(s_xws, 7)
            step(dve.tensor_tensor(prop[0:LO], prop[0:LO], dinv[0:LO, :, None].to_broadcast([LO, HI, D]), ALU.mult))

            def three_parts(to, of, rest):
                step(dve.tensor_copy(to(0), of))
                step(dve.tensor_tensor(rest, of, to(0), ALU.subtract))
                step(dve.tensor_copy(to(1), rest))
                step(dve.tensor_tensor(to(2), rest, to(1), ALU.subtract))

            rest1 = u2[0:LO, 0:2 * HI * D].bitcast(fp32).rearrange("p (h d) -> p h d", h=HI)
            three_parts(lambda k: split1[0:LO, :, k * D:(k + 1) * D], prop[0:LO, :, :], rest1)
            dve.nop().then_inc(s_prop, 1)

            def hop_sum(q, n):
                dve.wait_ge(s_hop, n + 1)
                step(dve.tensor_reduce(tmp[0:LO, 0, :], ps[0:LO, n % 2, 0:3 * D].rearrange("p (k d) -> p d k", k=3), axis=AX.X, op=ALU.add))
                dve.nop().then_inc(s_hopfree, 1)
                step(dve.tensor_tensor(tmp[0:LO, 1, :], tmp[0:LO, 0, :], prop[0:LO, q, :], ALU.add))

            for q in range(HI):
                hop_sum(q, q)
                step(dve.tensor_scalar(prop[0:LO, q, :], tmp[0:LO, 1, :], dinv2[0:LO, q:q + 1], None, ALU.mult))
                three_parts(lambda k: split2[0:LO, q, k * D:(k + 1) * D], prop[0:LO, q, :], tmp[0:LO, 2, :])
                dve.nop().then_inc(s_split2, 1)
            dve.wait_ge(s_bias, 32)
            def self_part(q):
                step(dve.tensor_tensor(xs[0:LO, q, :], x1[0:LO, q % 2, 0, :], biasvec[0:LO, :], ALU.add))
                dve.wait_ge(s_selfps, q + 1)
                dve.tensor_tensor(xs[0:LO, q, :], ps[0:LO, 7, 0:D], xs[0:LO, q, :], ALU.add).then_inc(s_selfsb, 1)

            for q in range(HI):
                hop_sum(q, HI + q)
                step(dve.scalar_tensor_tensor(tmp[0:LO, 0, :], tmp[0:LO, 1, :], dinv[0:LO, q:q + 1], bvec[0:LO, :], ALU.mult, ALU.add))
                step(dve.scalar_tensor_tensor(tmp[0:LO, 1, :], tmp[0:LO, 0, :], 0.0, xs[0:LO, q, :], ALU.max, ALU.add))
                step(dve.bn_stats(stats[0:LO, :], tmp[0:LO, 1, :]))
                dve.bn_aggr(mv[0:LO, :], stats[0:LO, :]).then_inc(s_var, 1)
                dve.wait_ge(s_std, q + 2)
                step(dve.reciprocal(rstd[0:LO, q % 2:q % 2 + 1], rstd[0:LO, q % 2:q % 2 + 1]))
                if q >= 2:
                    dve.wait_ge(s_x1ps, q - 1)
                dve.tensor_scalar(x1[0:LO, q % 2, :, :], tmp[0:LO, 1:2, :].to_broadcast([LO, 2, D]), mv[0:LO, 0:1], rstd[0:LO, q % 2:q % 2 + 1], ALU.subtract, ALU.mult).then_inc(s_x1, 1)
                dve.wait_ge(s_x1, q + 1)
                if q >= 1:
                    self_part(q - 1)
            self_part(HI - 1)

            m2 = dve.value_load(passes[0:1, 1:2], min_val=1, max_val=N)
            dve.memset(acc, 0.0).then_inc(s_accz, 1)
            dve.wait_ge(s_const, 4)
            dve.wait_ge(s_accz, 1)
            dve.sem_inc(msg_free, 2)
            with dve.Fori(0, m2) as v:
                def one_hots2(g, s, n):
                    dve.wait_ge(msg_done, n + 2)
                    dve.tensor_tensor(oh2[:, s, :, :], iota_2[:, None, :].to_broadcast([P, J, KW2]),
                                      key2[:, :, bass.ds(g, 1)].to_broadcast([P, J, KW2]), ALU.is_equal).then_inc(oh2_ready, 1)

                def add_message(g, s, done):
                    col = dve.value_load(columns[0:1, bass.ds(g, 1)], min_val=0, max_val=HI * D)
                    dve.wait_ge(msg_done, done + 4)
                    dve.wait_ge(msg_free, done + 1)
                    a = acc[0:LO, bass.ds(col, Q2 * D)].rearrange("p (q d) -> p q d", q=Q2)
                    dve.tensor_tensor(a, a, ps[0:LO, 2 * s:2 * s + 2, 0:D], ALU.add).then_inc(msg_free, 1)

                one_hots2(0, 0, v * NG + 1)
                with dve.Fori(0, NPAIR - 1) as i:
                    g = i * 2
                    one_hots2(g + 1, 1, v * NG + g + 2)
                    add_message(g, 0, v * NG + g + 1)
                    one_hots2(g + 2, 0, v * NG + g + 3)
                    add_message(g + 1, 1, v * NG + g + 2)
                one_hots2(NG - 1, 1, v * NG + NG)
                add_message(NG - 2, 0, v * NG + NG - 1)
                add_message(NG - 1, 1, v * NG + NG)
                dve.tensor_scalar(key2[:], key2[:], -float(KW2), None, ALU.add).then_inc(s_accz, 1)
                dve.tensor_scalar(columns, columns, float(Q2 * D), float(HI * D), ALU.add, ALU.min).then_inc(s_accz, 1)
                dve.wait_ge(s_accz, v * 2 + 3)

            a3 = acc[0:LO, 0:HI * D].rearrange("p (h d) -> p h d", h=HI)
            yv, y2v = y[0:LO], y2[0:LO]
            step(dve.tensor_tensor(yv, a3, rind[0:LO, :, None].to_broadcast([LO, HI, D]), ALU.mult))
            step(dve.tensor_tensor(yv, yv, xs[0:LO], ALU.add))
            step(dve.tensor_reduce(mean[0:LO, :], yv, axis=AX.X, op=ALU.add))
            step(dve.tensor_scalar(mean[0:LO, :], mean[0:LO, :], 1.0 / D, None, ALU.mult))
            step(dve.tensor_tensor(yv, yv, mean[0:LO, :, None].to_broadcast([LO, HI, D]), ALU.subtract))
            step(dve.tensor_tensor(y2v, yv, yv, ALU.mult))
            step(dve.tensor_reduce(var[0:LO, :], y2v, axis=AX.X, op=ALU.add))
            dve.nop().then_inc(s_fv, 1)
            dve.wait_ge(s_fs, 1)
            step(dve.reciprocal(var[0:LO, :], var[0:LO, :]))
            step(dve.tensor_tensor(yv, yv, var[0:LO, :, None].to_broadcast([LO, HI, D]), ALU.mult))
            dve.nop().then_inc(s_fin, 1)


_INS = ['x', 'src', 'dst', 'edge_type_32', 'L0_gnn_W', 'L0_gnn_b', 'L1_gnn_basis', 'L1_gnn_coeff', 'L1_gnn_self_weight', 'L1_gnn_bias']


def kernel(**inputs):
    import numpy as _np
    import concourse.bacc as _bacc
    from concourse import mybir as _mybir
    from concourse.bass_utils import run_bass_kernel_spmd as _run

    nc = _bacc.Bacc("TRN2", target_bir_lowering=False, num_devices=1)
    arrays, args = {}, []
    for name in _INS:
        a = _np.ascontiguousarray(inputs[name])
        arrays[f"in_{name}"] = a
        args.append(nc.dram_tensor(f"in_{name}", a.shape, _mybir.dt.from_np(a.dtype), kind="ExternalInput").ap())
    out = nc.dram_tensor("out", (N, D), _mybir.dt.float32, kind="ExternalOutput").ap()
    build(nc, *args, out)
    r = _run(nc, [arrays], core_ids=[0])
    return r.results[0]["out"]
```

```python
from contextlib import ExitStack

import concourse.bass as bass
from concourse import mybir

N, D, E, R, B = 3125, 64, 103125, 32, 30
LO, HI = 125, 25
P = 128
J = 4
GE = J * P
NG = -(-E // GE)
C = -(-NG // P)
GP = C * P
NPAIR = NG // 2
AHEAD = 3
STEADY = (NG - AHEAD) // 4
NQUAD = NG // 4
ONE = LO
W = 18
KW = W * HI
ND = N + 19
Q2 = 2
KW2 = Q2 * LO
ROUND = 12582912.0
FAR = -1048576.0
EPS = 1e-5
TOPVAL = 1024.0
TINY = 1e-30
EXACT = 2048.0
DEG, HOP1, HOP2 = range(3)
HALVES = ((0, HI // 2 + 1), (HI // 2 + 1, HI))
RW = (R + 1) * D
KEYS, LOS, KEY2, ROWS = range(4)


class SumSignals:

    def __init__(self, sem, name):
        self.made = sem(name + "_made")
        self.stored = sem(name + "_stored")
        self.iota = sem(name + "_iota")
        self.idx_ready = sem(name + "_idx_ready")
        self.taken = sem(name + "_taken")
        self.got = [sem(f"{name}_got{i}") for i in range(4)]
        self.oh_ready = sem(name + "_oh_ready")
        self.done = sem(name + "_done")
        self.free = sem(name + "_free")
        self.acc = sem(name + "_acc")
        self.step = sem(name + "_step")
        self.cleared = sem(name + "_cleared")


def build(nc, x, src, dst, typ, w, b, basis, coeff, selfw, bias, out):
    fp32, i32 = mybir.dt.float32, mybir.dt.int32
    fp16 = mybir.dt.float16
    ALU, ACT, AX = mybir.AluOpType, mybir.ActivationFunctionType, mybir.AxisListType
    ctx = ExitStack()
    with ctx:
        def sb(name, shape, dt):
            return ctx.enter_context(nc.sbuf_tensor(name, shape, dt))

        def sem(name):
            return ctx.enter_context(nc.semaphore(name))

        rel_dram = nc.dram_tensor("rel_dram", (R, D, D), fp32, kind="Internal").ap()
        feature_dram = nc.dram_tensor("feature_dram", (N, D), fp32, kind="Internal").ap()
        table = nc.dram_tensor("table", (N * R, D), fp32, kind="Internal").ap()

        adj = sb("adj", [P, HI, ND], fp16)
        adj_flat = adj[:, :, :].rearrange("p h n -> p (h n)")

        def inside(first_hi, words, dt=fp32):
            start = first_hi * ND
            return adj_flat[:, start:start + 2 * words].bitcast(dt)

        TM = C * GE
        TAIL = 12

        def tm(n, dt=fp32):
            start = 18 * ND + n * 2 * TM
            return adj_flat[:, start:start + 2 * TM].bitcast(dt)
        raw = [tm(n, i32) for n in range(3)]
        srcF, typF, keyF, key2F, hiF, dstF = (tm(n) for n in range(3, 9))
        eid = adj_flat[:, 18 * ND + 9 * 2 * TM:18 * ND + 9 * 2 * TM + 2 * GE].bitcast(fp32)
        LISTS = 18 * ND + 3 * 2 * TM
        zero_first = adj_flat[:, 0:TAIL * ND].bitcast(fp32)
        zero_weights = adj_flat[:, TAIL * ND:18 * ND].bitcast(fp32)
        zero_raw = adj_flat[:, 18 * ND:LISTS].bitcast(fp32)
        zero_rest = adj_flat[:, LISTS + 4 * 2 * TM:HI * ND].bitcast(fp32)
        zero_lists = [adj_flat[:, LISTS + k * 4 * TM:LISTS + (k + 1) * 4 * TM].bitcast(fp32) for k in range(2)]
        basis_sb = inside(12, D * D)
        rel_sb = inside(15, D * D)
        oh2 = inside(0, 2 * J * KW2).rearrange("p (s j k) -> p s j k", s=2, j=J)
        got = inside(13, 4 * J * D).rearrange("p (s j d) -> p s j d", s=4, j=J)
        acc = inside(4, (HI + Q2) * D)
        y = inside(7, HI * D).rearrange("p (h d) -> p h d", h=HI)
        iota_2 = inside(9, KW2)
        y2 = inside(10, HI * D).rearrange("p (h d) -> p h d", h=HI)
        sources = inside(12, J * GP).rearrange("p (j g) -> p j g", j=J)
        key2_kept = inside(15, J * GP).rearrange("p (j g) -> p j g", j=J)
        columns_kept = inside(17, GP, i32)[32:33, :]
        ones = inside(18, HI * D).rearrange("p (h d) -> p h d", h=HI)

        u0 = sb("u0", [P, 2 * RW], fp16)
        split1 = u0[:, 0:HI * 2 * D].rearrange("p (h d) -> p h d", h=HI)
        xT = u0[0:D, 0:2 * J * P * 2].bitcast(fp32).rearrange("p (s n) -> p s n", s=2)
        rel16 = u0[:, :].rearrange("p (k n) -> p k n", k=2)
        u1 = sb("u1", [P, 4 * J * GP], fp16)
        split2 = u1[:, 0:HI * 2 * D].rearrange("p (h d) -> p h d", h=HI)
        keys = u1[:, 0:2 * J * GP].bitcast(fp32).rearrange("p (j g) -> p j g", j=J)
        los = u1[:, 2 * J * GP:4 * J * GP].bitcast(fp32).rearrange("p (j g) -> p j g", j=J)
        head = sb("head", [P, 2 * D + B + R], fp32)
        bvec, biasvec = head[:, 0:D], head[:, D:2 * D]
        wt, wsb = head[0:D, 0:D], head[0:D, D:2 * D]
        cfsb, cft = head[0:R, 2 * D:2 * D + B], head[0:B, 2 * D + B:]
        key2 = sb("key2", [P, J, GP], fp32)
        rows = sb("rows", [P, J, GP], fp32)
        prop = sb("prop", [P, HI, D], fp32)
        xs = sb("xs", [P, HI, D], fp32)
        u2 = sb("u2", [P, 2 * J * (KW + P) + J * LO], fp16)
        relF = u2[:, 0:2 * RW].bitcast(fp32)
        away3 = sb("away3", [P, J * LO], fp16)
        ohk = [u[:, k * J * KW:(k + 1) * J * KW].rearrange("p (j k) -> p j k", j=J) for u in (u2, u0) for k in range(2)]
        ohl = u2[:, 2 * J * KW:2 * J * (KW + P)].rearrange("p (s j k) -> p s j k", s=2, j=J)
        away = [u[:, start:start + J * LO].rearrange("p (j k) -> p j k", j=J)
                for u, start in ((u0, 2 * J * KW), (u2, 2 * J * (KW + P)), (away3, 0))]
        stage = u2[:, 0:4 * 2 * 512].bitcast(fp32).rearrange("p (s n) -> p s n", s=4)
        iota_k = sb("iota_k", [P, KW], fp16)
        ident = sb("ident", [P, P], fp32)
        sm = sb("sm", [P, 6], fp32)
        sm2 = sb("sm2", [P, 6], fp32)
        tabl = sb("tabl", [D, GP], i32)
        bases, columns = tabl[0:1, :], tabl[32:33, :]
        cnts = sb("cnts", [1, 2], fp32)
        passes = sb("passes", [1, 3], i32)
        dinv = sb("dinv", [P, HI], fp32)
        dinv2 = sb("dinv2", [P, HI], fp32)
        rind = sb("rind", [P, HI], fp32)
        divisor = sb("divisor", [P, HI], fp32)
        deg = sb("deg", [P, HI], fp32)
        u3 = sb("u3", [P, 7 * D], fp32)
        tmp = u3[:, 0:3 * D].rearrange("p (n d) -> p n d", n=3)
        x1 = u3[:, 3 * D:5 * D].rearrange("p (s d) -> p s d", s=2)
        x16 = u3[:, 5 * D:7 * D].bitcast(fp16).rearrange("p (s k d) -> p s k d", s=2, k=2)
        x1T = u2[:, 4 * 2 * 512:4 * 2 * 512 + 2 * P].rearrange("p (s n) -> p s n", s=2)
        ident16 = sb("ident16", [P, P], fp16)
        onesrow = u3[0:1, 3 * D:3 * D + P]
        top = sb("top", [P, 2], fp32)
        one_top = sb("one_top", [1, 4], fp32)
        scales = sb("scales", [P, 4], fp32)
        dinv_s = sb("dinv_s", [P, HI], fp32)
        stats = sb("stats", [P, 6], fp32)
        mv = sb("mv", [P, 4], fp32)
        rstd = sb("rstd", [P, 2], fp32)
        idx = sb("idx", [P, 4, J], i32)
        block_counts = u0[0:HI, 0:N]
        one_each = ohl[0:HI, 0, 0, ONE:ONE + 1]
        mean = inside(6, 2 * HI)[:, 0:HI]
        var = inside(6, 2 * HI)[:, HI:]
        epsv = sb("epsv", [P, 1], fp32)
        ps = ctx.enter_context(nc.psum_tensor("ps", [P, 8, 512], fp32))
        ps16 = ps[:, 2, 0:P].bitcast(fp16)

        src_loaded, dst_loaded, types_loaded = sem("src_loaded"), sem("dst_loaded"), sem("types_loaded")
        padding_set = sem("padding_set")
        x_loaded, w_coeff_loaded, basis_loaded, rel_loaded, rel_stored, biases_loaded = (sem(n) for n in ("x_loaded", "w_coeff_loaded", "basis_loaded", "rel_loaded", "rel_stored", "biases_loaded"))
        first_constants_set, ident_made, constants_made, eid_made = (sem(n) for n in ("first_constants_set", "ident_made", "constants_made", "eid_made"))
        w_coeff_transposed, w_coeff_copied, rel_product, rel_copied, xT_transposed, xT_copied, xw_product, xw_copied = (sem(n) for n in ("w_coeff_transposed", "w_coeff_copied", "rel_product", "rel_copied", "xT_transposed", "xT_copied", "xw_product", "xw_copied"))
        dve_step = sem("dve_step")
        keys_made, keys_transposed, keys_copied, bases_transposed, tables_made, counts_zeroed = (sem(n) for n in ("keys_made", "keys_transposed", "keys_copied", "bases_transposed", "tables_made", "counts_zeroed"))
        key_ready, win_done, win_free = (sem(n) for n in ("key_ready", "win_done", "win_free"))
        degrees_product, counts_done, hop1_operand_ready, hop_product, hop_read, hop2_operand_ready, variance_ready, root_ready = (sem(n) for n in ("degrees_product", "counts_done", "hop1_operand_ready", "hop_product", "hop_read", "hop2_operand_ready", "variance_ready", "root_ready"))
        x1_ready, x1_transposed, x1T_copied, table_product, table_copied, self_product, self_added = (sem(n) for n in ("x1_ready", "x1_transposed", "x1T_copied", "table_product", "table_copied", "self_product", "self_added"))
        table_stored = [sem(f"table_stored{i}") for i in range(4)]
        next_windows_set, many_ready, many_transposed, flag_ready = (sem(n) for n in ("next_windows_set", "many_ready", "many_transposed", "flag_ready"))

        MSG = SumSignals(sem, "msg")
        EDGE = [SumSignals(sem, n) for n in ("deg", "hop1", "hop2")]
        counts_moved, degrees_redone, features_scaled, first_part_made, roots_redone, lo_ready, away_ready, ones_column_set = (sem(n) for n in ("counts_moved", "degrees_redone", "features_scaled", "first_part_made", "roots_redone", "lo_ready", "away_ready", "ones_column_set"))
        ident16_made, rel16_made, top_ready, top_moved, one_top_ready, scale_ready = (sem(n) for n in ("ident16_made", "rel16_made", "top_ready", "top_moved", "one_top_ready", "scale_ready"))
        last_root_ready, last_norm_ready, squares_ready, half_normed, out_stored = sem("last_root_ready"), sem("last_norm_ready"), sem("squares_ready"), sem("half_normed"), sem("out_stored")

        block = ctx.enter_context(nc.Block())
        FULL = E // GE
        TOP = FULL - P
        LAST = E - FULL * GE

        @block.sync
        def _(sp):
            sp.wait_ge(padding_set, 3)
            for a, r, s in ((dst, raw[1], dst_loaded), (src, raw[0], src_loaded), (typ, raw[2], types_loaded)):
                v = r.rearrange("p (c e) -> p c e", c=C)
                sp.dma_start(v[:, 0, :], a[0:P * GE].rearrange("(p e) -> p e", p=P)).then_inc(s, 16)
                sp.dma_start(v[0:TOP, 1, :], a[P * GE:FULL * GE].rearrange("(p e) -> p e", e=GE)).then_inc(s, 16)
                sp.dma_start(v[TOP:TOP + 1, 1, 0:LAST], a[FULL * GE:E].rearrange("(p e) -> p e", p=1)).then_inc(s, 16)
            sp.wait_ge(rel_copied, 8)
            sp.dma_start(rel_dram.rearrange("r i o -> r (i o)"), rel_sb[0:R, :]).then_inc(rel_stored, 16)
            sp.wait_ge(rel_stored, 16)
            sp.wait_ge(xw_product, 7)
            sp.dma_start(bvec, b[None, :].to_broadcast([P, D])).then_inc(biases_loaded, 16)
            sp.dma_start(biasvec, bias[None, :].to_broadcast([P, D])).then_inc(biases_loaded, 16)
            sp.wait_ge(counts_done, 1)
            sp.dma_start(block_counts, adj[ONE:ONE + 1, :, 0:N]).then_inc(counts_moved, 16)
            sp.wait_ge(degrees_product, 1)
            for half in (relF[0:D], relF[D:2 * D]):
                sp.dma_start(half[:, 0:R * D].rearrange("i (r o) -> i r o", r=R), rel_dram.rearrange("r i o -> i r o")).then_inc(rel_loaded, 16)
                sp.dma_start(half[:, R * D:(R + 1) * D], selfw).then_inc(rel_loaded, 16)
            sp.wait_ge(flag_ready, 1)
            many = sp.value_load(passes[0:1, 2:3], min_val=0, max_val=1)
            for k, features in ((DEG, ones), (HOP1, prop), (HOP2, prop)):
                with sp.If(many != 0):
                    sp.wait_ge(EDGE[k].made, 1)
                    sp.dma_start(feature_dram.rearrange("(h l) d -> l h d", l=LO), features[0:LO, :, :]).then_inc(EDGE[k].stored, 16)
                    sp.wait_ge(EDGE[k].stored, 16)
            tv = table.rearrange("(n r) d -> n (r d)", r=R)
            for q in range(HI):
                for c in range(4):
                    sp.wait_ge(table_copied, 4 * q + c + 1)
                    sp.dma_start(tv[q * LO:(q + 1) * LO, c * 512:(c + 1) * 512], stage[0:LO, c, :]).then_inc(table_stored[c], 16)
            for k, h in enumerate(HALVES):
                sp.wait_ge(half_normed, k + 1)
                sp.dma_start(out.rearrange("(h l) d -> l h d", l=LO)[:, h[0]:h[1], :], y[0:LO, h[0]:h[1], :]).then_inc(out_stored, 16)
            sp.wait_ge(out_stored, 32)

        @block.gpsimd
        def _(pool):
            pool.memset(raw[0], 0).then_inc(padding_set, 1)
            pool.memset(raw[1], N - 1).then_inc(padding_set, 1)
            pool.memset(raw[2], 0).then_inc(padding_set, 1)
            pool.memset(ident[:], 0.0).then_inc(first_constants_set, 1)
            pool.wait_ge(first_constants_set, 1)
            pool.affine_select(out=ident[:], in_=ident[:], compare_op=ALU.not_equal, fill=1.0, base=0,
                               pattern=[[-1, P]], channel_multiplier=1).then_inc(ident_made, 1)
            pool.iota(eid, [[1, GE]], base=P * GE - E, channel_multiplier=GE,
                      allow_small_or_imprecise_dtypes=True).then_inc(eid_made, 1)
            pool.iota(iota_k[:], [[1, KW]], base=0, channel_multiplier=0, allow_small_or_imprecise_dtypes=True).then_inc(constants_made, 1)
            pool.memset(onesrow, 1.0).then_inc(first_constants_set, 1)
            pool.memset(ohl, 0.0).then_inc(first_constants_set, 1)
            pool.wait_ge(first_constants_set, 3)
            pool.memset(ohl[:, :, :, ONE:ONE + 1], 1.0).then_inc(ones_column_set, 1)
            pool.memset(epsv[:], EPS).then_inc(constants_made, 1)
            pool.memset(zero_first, 0.0).then_inc(counts_zeroed, 1)
            pool.wait_ge(rel_stored, 16)
            pool.memset(zero_weights, 0.0).then_inc(counts_zeroed, 1)
            pool.wait_ge(keys_made, 3)
            pool.memset(zero_raw, 0.0).then_inc(counts_zeroed, 1)
            pool.memset(zero_rest, 0.0).then_inc(counts_zeroed, 1)
            pool.wait_ge(keys_transposed, 4)
            pool.memset(zero_lists[0], 0.0).then_inc(counts_zeroed, 1)

            def gather_all(S, rows_of):
                m2 = pool.value_load(passes[0:1, 1:2], min_val=1, max_val=N)
                with pool.Fori(0, m2) as v:
                    def gather(g, s):
                        pool.wait_ge(S.idx_ready, v * NG + g + 1)
                        pool.sem_inc(S.taken, 1)
                        for j in range(J):
                            pool.indirect_dma_start(got[:, s, j, :], None, rows_of,
                                                    bass.IndirectOffsetOnAxis(ap=idx[:, s, j:j + 1], axis=0)).then_inc(S.got[s], 16)

                    with pool.Fori(0, NQUAD) as i:
                        for s in range(4):
                            gather(i * 4 + s, s)
                    for s in range(2):
                        gather(NQUAD * 4 + s, s)

            pool.wait_ge(flag_ready, 1)
            many = pool.value_load(passes[0:1, 2:3], min_val=0, max_val=1)
            for S in EDGE:
                with pool.If(many != 0):
                    pool.wait_ge(S.made, 1)
                    pool.iota(iota_2, [[1, KW2]], base=0, channel_multiplier=0, allow_small_or_imprecise_dtypes=True).then_inc(S.iota, 1)
                    pool.wait_ge(S.stored, 16)
                    gather_all(S, feature_dram)
            for c in range(4):
                pool.wait_ge(table_stored[c], 16 * HI)
            pool.iota(iota_2, [[1, KW2]], base=0, channel_multiplier=0, allow_small_or_imprecise_dtypes=True).then_inc(MSG.iota, 1)
            gather_all(MSG, table)

        @block.scalar
        def _(act):
            act.dma_start(wsb, w).then_inc(w_coeff_loaded, 16)
            act.dma_start(cfsb, coeff).then_inc(w_coeff_loaded, 16)
            act.dma_start(xs[0:LO, :, :], x.rearrange("(h l) d -> l h d", l=LO)).then_inc(x_loaded, 16)
            act.dma_start(basis_sb[0:B, :], basis.rearrange("b i o -> b (i o)")).then_inc(basis_loaded, 16)
            act.wait_ge(w_coeff_transposed, 2)
            act.copy(wt, ps[0:D, 0, 0:D]).then_inc(w_coeff_copied, 1)
            act.copy(cft, ps[0:B, 1, 0:R]).then_inc(w_coeff_copied, 1)
            for k in range(8):
                act.wait_ge(rel_product, k + 1)
                act.copy(rel_sb[0:R, k * 512:(k + 1) * 512], ps[0:R, 2 + k % 2, :]).then_inc(rel_copied, 1)

            def x_copy(k):
                n = min(4, HI - 4 * k)
                act.wait_ge(xT_transposed, k + 1)
                if k >= 2:
                    act.wait_ge(xw_product, k - 1)
                act.copy(xT[:, k % 2, 0:n * LO], ps[0:D, k % 2, 0:n * LO]).then_inc(xT_copied, 1)

            for k in range(7):
                n = min(4, HI - 4 * k)
                if k == 0:
                    x_copy(0)
                if k < 6:
                    x_copy(k + 1)
                act.wait_ge(xw_product, k + 1)
                act.copy(prop[0:LO, 4 * k:4 * k + n, :], ps[0:LO, 6 + k % 2, 0:n * D].rearrange("p (n d) -> p n d", n=n)).then_inc(xw_copied, 1)
            act.wait_ge(tables_made, 1)
            m1 = act.value_load(passes[0:1, 0:1], min_val=1, max_val=N)
            act.wait_ge(keys_copied, 4)
            act.wait_ge(constants_made, 2)
            act.wait_ge(ones_column_set, 1)
            act.sem_inc(lo_ready, 4)
            with act.Fori(0, m1) as v:
                def distance(g, s):
                    act.wait_ge(lo_ready, v * NG + g + 2)
                    for j in range(J):
                        last = act.activation(away[s % 3][:, j, :], iota_k[:, 0:LO], ACT.Abs, bias=los[:, j, bass.ds(g, 1)])
                    last.then_inc(away_ready, 1)

                def one_hot(g, s):
                    act.wait_ge(away_ready, v * NG + g + 1)
                    act.wait_ge(win_done, v * NG + g + 3)
                    act.activation(ohl[:, s % 2, :, 0:LO], away[s % 3], ACT.Relu, scale=-1.0, bias=1.0).then_inc(lo_ready, 1)

                act.wait_ge(lo_ready, v * NG + 4)
                distance(0, 0)
                with act.Fori(0, NG // 6) as i:
                    for s in range(6):
                        distance(i * 6 + s + 1, s + 1)
                        one_hot(i * 6 + s, s)
                for g in range(NG // 6 * 6, NG):
                    if g + 1 < NG:
                        distance(g + 1, g + 1)
                    one_hot(g, g)

            def number_all(S, of):
                m2 = act.value_load(passes[0:1, 1:2], min_val=1, max_val=N)
                with act.Fori(0, m2) as v:
                    def number(g, s):
                        act.wait_ge(S.done, v * NG + g + 1)
                        act.copy(idx[:, s, :], of[:, :, bass.ds(g, 1)].rearrange("p j o -> p (j o)")).then_inc(S.idx_ready, 1)

                    act.wait_ge(S.done, v * NG + 4)
                    with act.Fori(0, NQUAD) as i:
                        for s in range(4):
                            number(i * 4 + s, s)
                    for s in range(2):
                        number(NQUAD * 4 + s, s)

            act.wait_ge(variance_ready, 1)
            act.activation(dinv[:], deg[:], ACT.Sqrt).then_inc(root_ready, 1)
            act.wait_ge(flag_ready, 1)
            many = act.value_load(passes[0:1, 2:3], min_val=0, max_val=1)
            for k in (DEG, HOP1, HOP2):
                with act.If(many != 0):
                    act.wait_ge(EDGE[k].made, 1)
                    number_all(EDGE[k], sources)
                    if k == DEG:
                        act.wait_ge(degrees_redone, 1)
                        act.activation(dinv[:], deg[:], ACT.Sqrt).then_inc(roots_redone, 1)
                if k == DEG:
                    for c, (a, z) in enumerate(HALVES):
                        act.wait_ge(features_scaled, c + 1)
                        act.copy(split1[0:LO, a:z, 0:D], prop[0:LO, a:z, :]).then_inc(first_part_made, 1)
            act.wait_ge(hop_product, HI)
            act.wait_ge(rel_loaded, 64)
            act.wait_ge(scale_ready, 2)
            act.activation(rel16[:, 0, :], relF, ACT.Copy, scale=scales[:, 2:3]).then_inc(rel16_made, 1)
            def deviation(q):
                act.wait_ge(variance_ready, q + 2)
                act.activation(rstd[0:LO, q % 2:q % 2 + 1], mv[0:LO, 2 * (q % 2) + 1:2 * (q % 2) + 2], ACT.Sqrt, bias=epsv[0:LO, :]).then_inc(root_ready, 1)

            deviation(0)
            for q in range(HI):
                act.wait_ge(x1_transposed, q + 1)
                act.copy(x1T[:, q % 2, 0:LO], ps16[:, 0:LO]).then_inc(x1T_copied, 1)
                if q < HI - 1:
                    deviation(q + 1)
                for c in range(4):
                    act.wait_ge(table_product, 4 * q + c + 1)
                    if q >= 1:
                        act.wait_ge(table_stored[c], 16 * q)
                    act.activation(stage[0:LO, c, :], ps[0:LO, 3 + c, :], ACT.Copy, scale=scales[0:LO, 3:4]).then_inc(table_copied, 1)
            number_all(MSG, rows)
            def squares(k):
                h = HALVES[k]
                act.wait_ge(last_norm_ready, k + 1)
                act.activation(y2[0:LO, h[0]:h[1], :], y[0:LO, h[0]:h[1], :], ACT.Square).then_inc(squares_ready, 1)

            def deviations(k):
                g = var[0:LO, HALVES[k][0]:HALVES[k][1]]
                act.wait_ge(last_norm_ready, 3 + k)
                act.activation(g, g, ACT.Sqrt, bias=epsv[0:LO, :], scale=1.0 / D).then_inc(last_root_ready, 1)

            squares(0)
            squares(1)
            deviations(0)
            deviations(1)

        @block.tensor
        def _(pe):
            pe.wait_ge(ident_made, 1)
            pe.wait_ge(w_coeff_loaded, 32)
            pe.transpose(ps[0:D, 0, 0:D], wsb, ident[0:D, 0:D]).then_inc(w_coeff_transposed, 1)
            pe.transpose(ps[0:B, 1, 0:R], cfsb, ident[0:R, 0:R]).then_inc(w_coeff_transposed, 1)
            pe.wait_ge(w_coeff_copied, 2)
            pe.wait_ge(basis_loaded, 16)
            for k in range(8):
                if k >= 2:
                    pe.wait_ge(rel_copied, k - 1)
                pe.matmul(ps[0:R, 2 + k % 2, :], cft, basis_sb[0:B, k * 512:(k + 1) * 512], start=True, stop=True).then_inc(rel_product, 1)
            pe.wait_ge(rel_copied, 8)
            def greatest(k):
                pe.wait_ge(top_ready, k + 1)
                pe.transpose(ps[0:1, 2, 0:P], top[:, k:k + 1], ident[:]).then_inc(top_moved, 1)
                pe.wait_ge(one_top_ready, k + 1)
                pe.matmul(ps[:, 2, 0:2], onesrow, one_top[0:1, 2 * k:2 * k + 2], start=True, stop=True).then_inc(top_moved, 1)

            pe.wait_ge(keys_made, 1)
            for k in range(6):
                last = pe.transpose(ps[0:1, k // 4, (k % 4) * P:(k % 4 + 1) * P], sm[:, k:k + 1], ident[:])
            last.then_inc(bases_transposed, 1)
            for k, (arr, need) in enumerate(((srcF, 2), (typF, 2), (keyF, 3), (key2F, 3))):
                pe.wait_ge(keys_made, need)
                v = arr.rearrange("p (c j e) -> p c j e", c=C, j=J)
                for c in range(C):
                    t = 2 + (2 * k + c) % 4
                    if 2 * k + c >= 4 and c == 0:
                        pe.wait_ge(keys_copied, k - 1)
                    for j in range(J):
                        last = pe.transpose(ps[:, t, j * P:(j + 1) * P], v[:, c, j, :], ident[:])
                    last.then_inc(keys_transposed, 1)

            pe.wait_ge(x_loaded, 16)

            def x_transpose(k):
                n = min(4, HI - 4 * k)
                if k >= 2:
                    pe.wait_ge(xT_copied, k - 1)
                for m in range(n):
                    last = pe.transpose(ps[0:D, k % 2, m * LO:(m + 1) * LO], xs[0:LO, 4 * k + m, :], ident[0:LO, 0:LO])
                last.then_inc(xT_transposed, 1)

            pe.wait_ge(tables_made, 1)
            x_transpose(0)
            for k in range(7):
                if k < 6:
                    x_transpose(k + 1)
                n = min(4, HI - 4 * k)
                pe.wait_ge(xT_copied, k + 1)
                if k >= 2:
                    pe.wait_ge(xw_copied, k - 1)
                for m in range(n):
                    last = pe.matmul(ps[0:LO, 6 + k % 2, m * D:(m + 1) * D], xT[:, k % 2, m * LO:(m + 1) * LO], wt, start=True, stop=True)
                last.then_inc(xw_product, 1)
            pe.wait_ge(tables_made, 1)
            m1 = pe.value_load(passes[0:1, 0:1], min_val=1, max_val=N)
            pe.wait_ge(keys_copied, 4)
            pe.sem_inc(win_done, 4)
            with pe.Fori(0, m1) as v:
                def window(g, s):
                    pe.wait_ge(lo_ready, v * NG + g + 5)
                    pe.wait_ge(key_ready, v * NG + g + 1)
                    pe.wait_ge(win_free, v * NG + g + 1)
                    for j in range(J):
                        last = pe.matmul(ps[:, s, 0:KW], ohl[:, s % 2, j, :], ohk[s][:, j, :], start=(j == 0), stop=(j == J - 1))
                    last.then_inc(win_done, 1)

                with pe.Fori(0, NQUAD) as i:
                    for s in range(4):
                        window(i * 4 + s, s)
                for s in range(2):
                    window(NQUAD * 4 + s, s)

            def add_up_all(S):
                m2 = pe.value_load(passes[0:1, 1:2], min_val=1, max_val=N)
                pe.sem_inc(S.done, 4)
                with pe.Fori(0, m2) as v:
                    def add_up(g, s, nth):
                        o = s % 2
                        pe.wait_ge(S.oh_ready, v * NG + g + 1)
                        pe.wait_ge(S.free, v * NG + g + 1)
                        pe.wait_ge(S.got[s], nth * (16 * J))
                        for j in range(J):
                            for h in range(Q2):
                                last = pe.matmul(ps[0:LO, 2 * o + h, 0:D], oh2[:, o, j, h * LO:(h + 1) * LO], got[:, s, j, :],
                                                 start=(j == 0), stop=(j == J - 1))
                        last.then_inc(S.done, 1)

                    with pe.Fori(0, NQUAD) as i:
                        for s in range(4):
                            add_up(i * 4 + s, s, v * (NQUAD + (s < 2)) + i + 1)
                    for s in range(2):
                        add_up(NQUAD * 4 + s, s, v * (NQUAD + 1) + NQUAD + 1)

            greatest(0)
            pe.wait_ge(scale_ready, 1)
            pe.wait_ge(counts_moved, 16)
            for q in range(HI):
                last = pe.matmul(ps[0:LO, 2, q:q + 1], block_counts[:, q * LO:(q + 1) * LO], one_each, start=True, stop=True)
            last.then_inc(degrees_product, 1)
            pe.wait_ge(many_ready, 1)
            pe.transpose(ps[0:1, 3, 0:P], top[:, 1:2], ident[:]).then_inc(many_transposed, 1)
            pe.wait_ge(flag_ready, 1)
            many = pe.value_load(passes[0:1, 2:3], min_val=0, max_val=1)

            def edge_by_edge(k):
                with pe.If(many != 0):
                    pe.wait_ge(EDGE[k].made, 1)
                    add_up_all(EDGE[k])
                    pe.wait_ge(EDGE[k].cleared, 1)

            edge_by_edge(DEG)

            def hop(q, parts, n):
                if n >= 2:
                    pe.wait_ge(hop_read, n - 1)
                for h in range(HI):
                    if n == 0 and h == HALVES[1][0]:
                        pe.wait_ge(hop1_operand_ready, 2)
                    last = pe.matmul(ps[0:LO, n % 2, 0:2 * D], adj[0:LO, h, q * LO:(q + 1) * LO], parts[0:LO, h, :], start=(h == 0), stop=(h == HI - 1))
                last.then_inc(hop_product, 1)

            pe.wait_ge(hop1_operand_ready, 1)
            edge_by_edge(HOP1)
            for q in range(HI):
                hop(q, split1, q)
                if q == 4:
                    greatest(1)
            pe.wait_ge(hop2_operand_ready, HI)
            edge_by_edge(HOP2)
            hop(0, split2, HI)
            hop(1, split2, HI + 1)
            for q in range(HI):
                if q == 0:
                    pe.wait_ge(rel16_made, 2)
                if q == 0:
                    pe.wait_ge(ident16_made, 1)
                pe.wait_ge(x1_ready, q + 1)
                pe.transpose(ps16[:, 0:LO], x16[0:LO, q % 2, :, :].rearrange("p t d -> p (t d)"), ident16[0:LO, 0:LO]).then_inc(x1_transposed, 1)
                if q < HI - 2:
                    hop(q + 2, split2, HI + q + 2)
                pe.wait_ge(x1T_copied, q + 1)
                for c in range(4):
                    if q >= 1:
                        pe.wait_ge(table_copied, 4 * (q - 1) + c + 1)
                    for k in range(2):
                        last = pe.matmul(ps[0:LO, 3 + c, :], x1T[:, q % 2, 0:LO], rel16[:, k, c * 512:(c + 1) * 512], start=(k == 0), stop=(k == 1))
                    last.then_inc(table_product, 1)
                if q >= 1:
                    pe.wait_ge(self_added, q)
                for k in range(2):
                    last = pe.matmul(ps[0:LO, 7, 0:D], x1T[:, q % 2, 0:LO], rel16[:, k, R * D:RW], start=(k == 0), stop=(k == 1))
                last.then_inc(self_product, 1)

            pe.wait_ge(self_added, HI)
            pe.wait_ge(table_copied, 4 * HI)
            add_up_all(MSG)

        @block.vector
        def _(dve):
            steps = [0]

            def step(ins):
                steps[0] += 1
                ins.then_inc(dve_step, 1)
                dve.wait_ge(dve_step, steps[0])

            def chunked(a, c):
                return a.rearrange("p (c e) -> p c e", c=C)[:, c, :]

            dve.wait_ge(ident_made, 1)
            dve.tensor_copy(ident16[:], ident[:]).then_inc(ident16_made, 1)
            dve.wait_ge(dst_loaded, 48)
            step(dve.tensor_copy(dstF, raw[1]))
            dve.tensor_reduce(sm[:, 0:2], dstF.rearrange("p (c e) -> p c e", c=C), axis=AX.X, op=ALU.min)
            step(dve.tensor_reduce(sm2[:, 0:2], dstF.rearrange("p (c e) -> p c e", c=C), axis=AX.X, op=ALU.max))
            step(dve.tensor_scalar(sm2[:, 2:4], sm[:, 0:2], 1.0 / LO, 0.5 / LO - 0.5, ALU.mult, ALU.add))
            step(dve.tensor_scalar(sm[:, 2:4], sm2[:, 2:4], ROUND, -ROUND, ALU.add, ALU.add))
            step(dve.tensor_scalar(sm2[:, 4:6], sm[:, 2:4], float(LO), None, ALU.mult))
            step(dve.tensor_tensor(sm2[:, 2:4], sm2[:, 0:2], sm[:, 0:2], ALU.subtract))
            step(dve.tensor_tensor(sm2[:, 0:2], sm2[:, 0:2], sm2[:, 4:6], ALU.subtract))
            step(dve.tensor_reduce(sm[:, 4:5], sm2[:, 2:4], axis=AX.X, op=ALU.max))
            dve.tensor_reduce(sm[:, 5:6], sm2[:, 0:2], axis=AX.X, op=ALU.max).then_inc(keys_made, 1)
            dve.wait_ge(src_loaded, 48)
            step(dve.tensor_copy(srcF, raw[0]))
            step(dve.tensor_scalar(keyF, srcF, 1.0 / LO, 0.5 / LO - 0.5, ALU.mult, ALU.add))
            step(dve.tensor_scalar(hiF, keyF, ROUND, -ROUND, ALU.add, ALU.add))
            dve.wait_ge(types_loaded, 48)
            step(dve.tensor_copy(typF, raw[2]))
            step(dve.scalar_tensor_tensor(typF, srcF, float(R), typF, ALU.mult, ALU.add))
            step(dve.scalar_tensor_tensor(srcF, hiF, float(LO), srcF, ALU.mult, ALU.subtract))
            dve.nop().then_inc(keys_made, 1)
            for c in range(C):
                dve.tensor_scalar(chunked(key2F, c), chunked(dstF, c), sm2[:, 4 + c:5 + c], None, ALU.subtract)
                step(dve.tensor_scalar(chunked(keyF, c), chunked(dstF, c), sm[:, c:c + 1], None, ALU.subtract))
            dve.wait_ge(eid_made, 1)
            step(dve.scalar_tensor_tensor(keyF, keyF, float(HI), hiF, ALU.mult, ALU.add))
            step(dve.tensor_scalar(eid, eid, 0.0, FAR, ALU.is_ge, ALU.mult))
            dve.tensor_tensor(chunked(keyF, 1), chunked(keyF, 1), eid, ALU.add)
            step(dve.tensor_tensor(chunked(key2F, 1), chunked(key2F, 1), eid, ALU.add))
            dve.nop().then_inc(keys_made, 1)
            dve.wait_ge(bases_transposed, 1)
            dve.tensor_copy(bases, ps[0:1, 0, 0:GP])
            dve.tensor_scalar(columns, ps[0:1, 0, GP:2 * GP], float(D), None, ALU.mult)
            step(dve.tensor_reduce(cnts[:], ps[0:1, 1, 0:2 * P].rearrange("p (k n) -> p k n", k=2), axis=AX.X, op=ALU.max))
            dve.tensor_scalar(cnts[0:1, 0:1], cnts[0:1, 0:1], 1.0 / W, 0.5 / W - 0.5, ALU.mult, ALU.add)
            step(dve.tensor_scalar(cnts[0:1, 1:2], cnts[0:1, 1:2], 1.0 / KW2, 0.5 / KW2 - 0.5, ALU.mult, ALU.add))
            step(dve.tensor_scalar(cnts[:], cnts[:], ROUND, -ROUND, ALU.add, ALU.add))
            step(dve.tensor_scalar(passes[0:1, 0:2], cnts[:], 1.0, None, ALU.add))
            dve.nop().then_inc(tables_made, 1)
            for k, to in enumerate((los, rows, keys, key2)):
                for c in range(C):
                    dve.wait_ge(keys_transposed, 2 * k + c + 1)
                    last = dve.tensor_copy(to[:, :, c * P:(c + 1) * P],
                                           ps[:, 2 + (2 * k + c) % 4, :].rearrange("p (j n) -> p j n", j=J))
                step(last)
                dve.nop().then_inc(keys_copied, 1)
            dve.memset(zero_lists[1], 0.0).then_inc(counts_zeroed, 1)

            m1 = dve.value_load(passes[0:1, 0:1], min_val=1, max_val=N)
            dve.wait_ge(constants_made, 2)
            dve.wait_ge(counts_zeroed, 6)
            dve.wait_ge(xw_product, 7)
            dve.sem_inc(win_free, 4)
            with dve.Fori(0, m1) as v:
                def one_hots(g, s):
                    for j in range(J):
                        last = dve.tensor_scalar(ohk[s][:, j, :], iota_k[:], keys[:, j, bass.ds(g, 1)], None, ALU.is_equal)
                    last.then_inc(key_ready, 1)

                def bases_of(g, n):
                    return nc.values_load_multi_w_load_instructions(bases[0:1, bass.ds(g, n)], engines=[mybir.EngineType.DVE], min_val=0, max_val=N)[1]

                def add_window(g, s, done, base):
                    dve.wait_ge(win_done, done + 4)
                    dve.wait_ge(win_free, done + 3)
                    a = adj[:, :, bass.ds(base, W)]
                    dve.tensor_tensor(a, a, ps[:, s, 0:KW].rearrange("p (n h) -> p h n", h=HI), ALU.add).then_inc(win_free, 1)

                for g in range(AHEAD):
                    one_hots(g, g)
                with dve.Fori(0, STEADY) as i:
                    for s in range(4):
                        g = i * 4 + s
                        one_hots(g + AHEAD, (s + AHEAD) % 4)
                        if s == 0:
                            base = bases_of(g, 4)
                        add_window(g, s % 4, v * NG + g + 1, base[s])
                for g in range(4 * STEADY, NG):
                    base, = bases_of(g, 1)
                    if g + AHEAD < NG:
                        one_hots(g + AHEAD, (g + AHEAD) % 4)
                    add_window(g, g % 4, v * NG + g + 1, base)
                dve.tensor_scalar(keys, keys, -float(KW), None, ALU.add).then_inc(next_windows_set, 1)
                dve.tensor_scalar(bases, bases, float(W), float(N), ALU.add, ALU.min).then_inc(next_windows_set, 1)
                dve.wait_ge(next_windows_set, v * 2 + 2)
            step(dve.memset(deg[:], 1.0))
            dve.nop().then_inc(counts_done, 1)

            def magnitude(k, of, want):
                step(dve.tensor_reduce(top[:, k:k + 1] if want == P else top[0:want, k:k + 1], of, axis=AX.XY if len(of.shape) == 3 else AX.X, op=ALU.max, apply_absolute_value=True))
                dve.nop().then_inc(top_ready, 1)

            def scale(k):
                dve.wait_ge(top_moved, 2 * k + 1)
                a, c = one_top[0:1, 2 * k:2 * k + 1], one_top[0:1, 2 * k + 1:2 * k + 2]
                step(dve.tensor_reduce(a, ps[0:1, 2, 0:P], axis=AX.X, op=ALU.max))
                step(dve.tensor_scalar(c, a, TINY, 1.0 / TOPVAL, ALU.max, ALU.mult))
                step(dve.reciprocal(a, c))
                dve.nop().then_inc(one_top_ready, 1)
                dve.wait_ge(top_moved, 2 * k + 2)
                step(dve.tensor_copy(scales[:, 2 * k:2 * k + 2], ps[:, 2, 0:2]))
                dve.nop().then_inc(scale_ready, 1)

            dve.wait_ge(xw_copied, 7)
            step(dve.memset(top[:], 0.0))
            magnitude(0, prop[0:LO].rearrange("p h d -> p (h d)"), LO)
            scale(0)
            step(dve.tensor_scalar(prop[0:LO], prop[0:LO], scales[0:LO, 0:1], None, ALU.mult))

            a3 = acc[0:LO, 0:HI * D].rearrange("p (h d) -> p h d", h=HI)

            def sum_all(S):
                m2 = dve.value_load(passes[0:1, 1:2], min_val=1, max_val=N)
                dve.wait_ge(S.iota, 1)
                dve.sem_inc(S.free, 2)
                with dve.Fori(0, m2) as v:
                    def one_hots2(g, s, n):
                        dve.wait_ge(S.done, n + 2)
                        dve.tensor_tensor(oh2[:, s, :, :], iota_2[:, None, :].to_broadcast([P, J, KW2]),
                                          key2[:, :, bass.ds(g, 1)].to_broadcast([P, J, KW2]), ALU.is_equal).then_inc(S.oh_ready, 1)

                    def add_message(g, s, done):
                        col = dve.value_load(columns[0:1, bass.ds(g, 1)], min_val=0, max_val=HI * D)
                        dve.wait_ge(S.done, done + 4)
                        dve.wait_ge(S.free, done + 1)
                        a = acc[0:LO, bass.ds(col, Q2 * D)].rearrange("p (q d) -> p q d", q=Q2)
                        dve.tensor_tensor(a, a, ps[0:LO, 2 * s:2 * s + 2, 0:D], ALU.add).then_inc(S.free, 1)

                    one_hots2(0, 0, v * NG + 1)
                    with dve.Fori(0, NPAIR - 1) as i:
                        g = i * 2
                        one_hots2(g + 1, 1, v * NG + g + 2)
                        add_message(g, 0, v * NG + g + 1)
                        one_hots2(g + 2, 0, v * NG + g + 3)
                        add_message(g + 1, 1, v * NG + g + 2)
                    one_hots2(NG - 1, 1, v * NG + NG)
                    add_message(NG - 2, 0, v * NG + NG - 1)
                    add_message(NG - 1, 1, v * NG + NG)
                    dve.tensor_scalar(key2[:], key2[:], -float(KW2), None, ALU.add).then_inc(S.acc, 1)
                    dve.tensor_scalar(columns, columns, float(Q2 * D), float(HI * D), ALU.add, ALU.min).then_inc(S.acc, 1)
                    dve.wait_ge(S.acc, v * 2 + 2)

            dve.wait_ge(degrees_product, 1)
            step(dve.tensor_scalar(deg[0:LO, :], ps[0:LO, 2, 0:HI], 1.0, None, ALU.add))
            dve.nop().then_inc(variance_ready, 1)
            step(dve.tensor_scalar(divisor[0:LO, :], ps[0:LO, 2, 0:HI], 1.0, None, ALU.max))
            step(dve.tensor_reduce(top[0:LO, 1:2], divisor[0:LO, :], axis=AX.X, op=ALU.max))
            step(dve.tensor_scalar(top[0:LO, 1:2], top[0:LO, 1:2], EXACT, None, ALU.is_ge))
            dve.nop().then_inc(many_ready, 1)
            dve.wait_ge(many_transposed, 1)
            step(dve.tensor_reduce(cnts[0:1, 0:1], ps[0:1, 3, 0:P], axis=AX.X, op=ALU.max))
            step(dve.tensor_copy(passes[0:1, 2:3], cnts[0:1, 0:1]))
            dve.nop().then_inc(flag_ready, 1)
            many = dve.value_load(passes[0:1, 2:3], min_val=0, max_val=1)
            dve.wait_ge(root_ready, 1)

            def edge_by_edge(k, use):
                with dve.If(many != 0):
                    S = EDGE[k]
                    count = [0]

                    def then(ins):
                        count[0] += 1
                        ins.then_inc(S.step, 1)
                        dve.wait_ge(S.step, count[0])

                    then(dve.tensor_scalar(sources, rows[:], 1.0 / R, 0.5 / R - 0.5, ALU.mult, ALU.add))
                    then(dve.tensor_scalar(sources, sources, ROUND, -ROUND, ALU.add, ALU.add))
                    then(dve.tensor_copy(key2_kept, key2[:]))
                    then(dve.tensor_copy(columns_kept, columns))
                    then(dve.memset(acc, 0.0))
                    if k == DEG:
                        then(dve.memset(ones, 1.0))
                    dve.nop().then_inc(S.made, 1)
                    sum_all(S)
                    then(dve.tensor_copy(key2[:], key2_kept))
                    then(dve.tensor_copy(columns, columns_kept))
                    use(then)
                    then(dve.memset(adj_flat[:, :], 0.0))
                    dve.nop().then_inc(S.cleared, 1)

            def use_degrees(then):
                degrees = a3[:, :, 0]
                then(dve.tensor_scalar(divisor[0:LO, :], degrees, 1.0, None, ALU.max))
                then(dve.tensor_scalar(deg[0:LO, :], degrees, 1.0, None, ALU.add))
                dve.nop().then_inc(degrees_redone, 1)
                dve.wait_ge(roots_redone, 1)

            def use_sums(then):
                then(dve.tensor_tensor(prop[0:LO], prop[0:LO], a3, ALU.add))

            edge_by_edge(DEG, use_degrees)
            step(dve.reciprocal(rind[0:LO, :], divisor[0:LO, :]))
            step(dve.reciprocal(dinv[:], dinv[:]))
            dve.tensor_tensor(dinv2[:], dinv[:], dinv[:], ALU.mult)
            dve.tensor_scalar(dinv_s[:], dinv[:], scales[:, 1:2], None, ALU.mult)

            def over_blocks(a):
                return a[0:LO, :, None].to_broadcast([LO, HI, D])

            def two_parts(to, of):
                step(dve.tensor_copy(to(0), of))
                step(dve.tensor_tensor(to(1), of, to(0), ALU.subtract))

            for a, z in HALVES:
                dve.tensor_tensor(prop[0:LO, a:z, :], prop[0:LO, a:z, :], dinv[0:LO, a:z, None].to_broadcast([LO, z - a, D]), ALU.mult).then_inc(features_scaled, 1)
            for c, (a, z) in enumerate(HALVES):
                dve.wait_ge(first_part_made, c + 1)
                step(dve.tensor_tensor(split1[0:LO, a:z, D:2 * D], prop[0:LO, a:z, :], split1[0:LO, a:z, 0:D], ALU.subtract))
                dve.nop().then_inc(hop1_operand_ready, 1)
            edge_by_edge(HOP1, use_sums)
            step(dve.tensor_tensor(prop[0:LO], prop[0:LO], over_blocks(dinv2), ALU.mult))

            def hop_sum(n):
                dve.wait_ge(hop_product, n + 1)
                step(dve.tensor_reduce(tmp[0:LO, 0, :], ps[0:LO, n % 2, 0:2 * D].rearrange("p (k d) -> p d k", k=2), axis=AX.X, op=ALU.add))
                dve.nop().then_inc(hop_read, 1)

            for q in range(HI):
                hop_sum(q)
                step(dve.scalar_tensor_tensor(prop[0:LO, q, :], tmp[0:LO, 0, :], dinv2[0:LO, q:q + 1], prop[0:LO, q, :], ALU.mult, ALU.add))
                two_parts(lambda k: split2[0:LO, q, k * D:(k + 1) * D], prop[0:LO, q, :])
                dve.nop().then_inc(hop2_operand_ready, 1)
                if q == 3:
                    dve.wait_ge(rel_loaded, 64)
                    magnitude(1, relF, P)
                if q == 4:
                    scale(1)
            edge_by_edge(HOP2, use_sums)
            dve.wait_ge(biases_loaded, 32)

            def self_part(q):
                step(dve.tensor_tensor(xs[0:LO, q, :], x1[0:LO, q % 2, :], biasvec[0:LO, :], ALU.add))
                dve.wait_ge(self_product, q + 1)
                dve.scalar_tensor_tensor(xs[0:LO, q, :], ps[0:LO, 7, 0:D], scales[0:LO, 3:4], xs[0:LO, q, :], ALU.mult, ALU.add).then_inc(self_added, 1)

            for q in range(HI):
                step(dve.scalar_tensor_tensor(prop[0:LO, q, :], prop[0:LO, q, :], dinv_s[0:LO, q:q + 1], bvec[0:LO, :], ALU.mult, ALU.add))
                hop_sum(HI + q)
                step(dve.scalar_tensor_tensor(tmp[0:LO, 0, :], tmp[0:LO, 0, :], dinv_s[0:LO, q:q + 1], prop[0:LO, q, :], ALU.mult, ALU.add))
                step(dve.scalar_tensor_tensor(tmp[0:LO, 1, :], tmp[0:LO, 0, :], 0.0, xs[0:LO, q, :], ALU.max, ALU.add))
                step(dve.bn_stats(stats[0:LO, :], tmp[0:LO, 1, :]))
                dve.bn_aggr(mv[0:LO, 2 * (q % 2):2 * (q % 2) + 2], stats[0:LO, :]).then_inc(variance_ready, 1)
                dve.wait_ge(root_ready, q + 2)
                step(dve.reciprocal(rstd[0:LO, q % 2:q % 2 + 1], rstd[0:LO, q % 2:q % 2 + 1]))
                step(dve.tensor_scalar(x1[0:LO, q % 2, :], tmp[0:LO, 1, :], mv[0:LO, 2 * (q % 2):2 * (q % 2) + 1], rstd[0:LO, q % 2:q % 2 + 1], ALU.subtract, ALU.mult))
                if q >= 2:
                    dve.wait_ge(x1_transposed, q - 1)
                two_parts(lambda k: x16[0:LO, q % 2, k, :], x1[0:LO, q % 2, :])
                dve.nop().then_inc(x1_ready, 1)
                if q == 0:
                    dve.wait_ge(rel16_made, 1)
                    step(dve.scalar_tensor_tensor(rel16[:, 1, :], relF, scales[:, 2:3], rel16[:, 0, :], ALU.mult, ALU.subtract))
                    dve.nop().then_inc(rel16_made, 1)
                if q >= 1:
                    self_part(q - 1)
            self_part(HI - 1)
            dve.wait_ge(self_added, HI)

            dve.memset(acc[:, HI * D:], 0.0)
            step(dve.tensor_tensor(a3, xs[0:LO], over_blocks(divisor), ALU.mult))
            sum_all(MSG)

            def over(a, h):
                return a[0:LO, h[0]:h[1], None].to_broadcast([LO, h[1] - h[0], D])

            for h in HALVES:
                yh, m = y[0:LO, h[0]:h[1], :], mean[0:LO, h[0]:h[1]]
                step(dve.tensor_reduce(m, a3[:, h[0]:h[1], :], axis=AX.X, op=ALU.add))
                step(dve.tensor_scalar(m, m, 1.0 / D, None, ALU.mult))
                step(dve.tensor_tensor(yh, a3[:, h[0]:h[1], :], over(mean, h), ALU.subtract))
                dve.nop().then_inc(last_norm_ready, 1)
            for k, h in enumerate(HALVES):
                g, rd = var[0:LO, h[0]:h[1]], rind[0:LO, h[0]:h[1]]
                dve.wait_ge(squares_ready, k + 1)
                step(dve.tensor_reduce(g, y2[0:LO, h[0]:h[1], :], axis=AX.X, op=ALU.add))
                step(dve.tensor_tensor(g, g, rd, ALU.mult))
                step(dve.tensor_tensor(g, g, rd, ALU.mult))
                dve.nop().then_inc(last_norm_ready, 1)
                dve.wait_ge(last_root_ready, k + 1)
                step(dve.reciprocal(g, g))
                step(dve.tensor_tensor(g, g, rd, ALU.mult))
                yh = y[0:LO, h[0]:h[1], :]
                step(dve.tensor_tensor(yh, yh, over(var, h), ALU.mult))
                dve.nop().then_inc(half_normed, 1)


_INS = ['x', 'src', 'dst', 'edge_type_32', 'L0_gnn_W', 'L0_gnn_b', 'L1_gnn_basis', 'L1_gnn_coeff', 'L1_gnn_self_weight', 'L1_gnn_bias']


def kernel(**inputs):
    import numpy as _np
    import concourse.bacc as _bacc
    from concourse import mybir as _mybir
    from concourse.bass_utils import run_bass_kernel_spmd as _run

    nc = _bacc.Bacc("TRN2", target_bir_lowering=False, num_devices=1)
    arrays, args = {}, []
    for name in _INS:
        a = _np.ascontiguousarray(inputs[name])
        arrays[f"in_{name}"] = a
        args.append(nc.dram_tensor(f"in_{name}", a.shape, _mybir.dt.from_np(a.dtype), kind="ExternalInput").ap())
    out = nc.dram_tensor("out", (N, D), _mybir.dt.float32, kind="ExternalOutput").ap()
    build(nc, *args, out)
    r = _run(nc, [arrays], core_ids=[0])
    return r.results[0]["out"]
```
